# Optimizing a Trainium2 kernel written in Bass

```python
import numpy as np
import jax
import jax.numpy as jnp

def _softmax(x, axis=-1):
    return jax.nn.softmax(x, axis=axis)

def _gelu(x):
    return jax.nn.gelu(x, approximate=True)

def _silu(x):
    return jax.nn.silu(x)

def _sigmoid(x):
    return jax.nn.sigmoid(x)

def _layernorm(x, axis=-1, eps=1e-05):
    m = jnp.mean(x, axis=axis, keepdims=True)
    v = jnp.var(x, axis=axis, keepdims=True)
    return (x - m) / jnp.sqrt(v + eps)

def _scatter_add(tgt, idx, src, axis=0):
    return tgt.at[idx].add(src)

def _segment_sum(src, seg, n):
    return jax.ops.segment_sum(src, seg, n)
kernel_name = 'mk_macaron_d2_jaxref_r8_4740b2'

def setup_inputs(seed: int=0):
    np.random.seed(seed)
    _w = jnp.asarray

    def _L0_attn_setup():
        import jax, jax.numpy as jnp
        import numpy as np
        B, T, C = (8, 512, 128)

        def _wkv(w_decay, u_first, k, v):
            w = -jnp.exp(w_decay)
            u = u_first
            kt = jnp.transpose(k, (1, 0, 2))
            vt = jnp.transpose(v, (1, 0, 2))
            a0 = jnp.zeros((k.shape[0], k.shape[2]), dtype=k.dtype)
            b0 = jnp.zeros_like(a0)
            p0 = jnp.full_like(a0, -1e+38)

            def step(carry, kv):
                a, b, p = carry
                k_t, v_t = kv
                q = jnp.maximum(p, u + k_t)
                e1 = jnp.exp(p - q)
                e2 = jnp.exp(u + k_t - q)
                y = (e1 * a + e2 * v_t) / (e1 * b + e2)
                q2 = jnp.maximum(p + w, k_t)
                f1 = jnp.exp(p + w - q2)
                f2 = jnp.exp(k_t - q2)
                return ((f1 * a + f2 * v_t, f1 * b + f2, q2), y)
            _, y = jax.lax.scan(step, (a0, b0, p0), (kt, vt))
            return jnp.transpose(y, (1, 0, 2))
        key = jax.random.key(seed)
        ks = jax.random.split(key, 5)
        scales = (jnp.arange(C, dtype=jnp.float32) / C).reshape(1, 1, C)
        return {'x': jax.random.normal(ks[0], (B, T, C), dtype=jnp.float32), 'time_decay': scales, 'time_first': scales, 'time_mix_k': scales, 'time_mix_v': scales, 'time_mix_r': scales, 'Wk': jax.random.normal(ks[1], (C, C), dtype=jnp.float32) / np.sqrt(C), 'Wv': jax.random.normal(ks[2], (C, C), dtype=jnp.float32) / np.sqrt(C), 'Wr': jax.random.normal(ks[3], (C, C), dtype=jnp.float32) / np.sqrt(C), 'Wo': jax.random.normal(ks[4], (C, C), dtype=jnp.float32) / np.sqrt(C)}
    _L0_attn_in = _L0_attn_setup()

    def _L0_ffn_setup():
        import jax, jax.numpy as jnp
        import numpy as np
        NEG_INF = -1e+30

        def _moe_forward(x, router_w, router_b, w1, b1, w2, b2, top_k=2):
            B, S, D = x.shape
            E = router_w.shape[1]
            logits = jnp.einsum('bsd,de->bse', x, router_w) + router_b
            top_vals, top_idx = jax.lax.top_k(logits, top_k)
            keep = jax.nn.one_hot(top_idx, E, dtype=logits.dtype).sum(-2) > 0
            sparse_logits = jnp.where(keep, logits, NEG_INF)
            gating = jax.nn.softmax(sparse_logits, axis=-1)
            xf = x.reshape(-1, D)
            gf = gating.reshape(-1, E)
            h = jax.nn.relu(jnp.einsum('td,edh->eth', xf, w1) + b1[:, None, :])
            y = jnp.einsum('eth,ehd->etd', h, w2) + b2[:, None, :]
            out = jnp.einsum('etd,te->td', y, gf)
            return out.reshape(B, S, D)
        key = jax.random.key(seed)
        ks = jax.random.split(key, 5)
        B, S, D, E, H = (2, 256, 128, 8, 512)
        scale = 0.02
        return {'x': jax.random.normal(ks[0], (B, S, D), dtype=jnp.float32), 'router_w': jax.random.normal(ks[1], (D, E), dtype=jnp.float32) * scale, 'router_b': jnp.zeros((E,), dtype=jnp.float32), 'w1': jax.random.normal(ks[2], (E, D, H), dtype=jnp.float32) * scale, 'b1': jnp.zeros((E, H), dtype=jnp.float32), 'w2': jax.random.normal(ks[3], (E, H, D), dtype=jnp.float32) * scale, 'b2': jnp.zeros((E, D), dtype=jnp.float32)}
    _L0_ffn_in = _L0_ffn_setup()

    def _L1_attn_setup():
        import jax, jax.numpy as jnp
        import numpy as np
        DIM = 128
        HEADS = 16
        DIM_HEAD = 64
        DIM_INNER = HEADS * DIM_HEAD

        def rms_norm(x, gamma):
            eps = 1e-12
            norm = jnp.maximum(jnp.linalg.norm(x, axis=-1, keepdims=True), eps)
            return x / norm * x.shape[-1] ** 0.5 * (gamma + 1.0)
        key = jax.random.key(seed)
        k1, k2, k3 = jax.random.split(key, 3)
        x = jax.random.normal(k1, (2, 256, DIM), dtype=jnp.float32)
        gamma = jnp.zeros((DIM,), dtype=jnp.float32)
        w_qkv = jax.random.normal(k2, (DIM, DIM_INNER * 3), dtype=jnp.float32) * DIM ** (-0.5)
        w_out = jax.random.normal(k3, (DIM_INNER, DIM), dtype=jnp.float32) * DIM_INNER ** (-0.5)
        return {'x': x, 'gamma': gamma, 'w_qkv': w_qkv, 'w_out': w_out}
    _L1_attn_in = _L1_attn_setup()

    def _L1_ffn_setup():
        import jax, jax.numpy as jnp
        import numpy as np
        DIM = 128
        HIDDEN = 384
        SCALE = 1.0 / 127.0

        def _dequant(w_int, dtype):
            return w_int.astype(dtype) * jnp.asarray(SCALE, dtype)
        key = jax.random.key(seed)
        k_x, k_g, k_u, k_d = jax.random.split(key, 4)
        x = jax.random.normal(k_x, (4, 256, DIM), dtype=jnp.float32)
        w_gate = jax.random.randint(k_g, (HIDDEN, DIM), -127, 128, dtype=jnp.int32)
        w_up = jax.random.randint(k_u, (HIDDEN, DIM), -127, 128, dtype=jnp.int32)
        w_down = jax.random.randint(k_d, (DIM, HIDDEN), -127, 128, dtype=jnp.int32)
        return {'x': x, 'w_gate': w_gate, 'w_up': w_up, 'w_down': w_down}
    _L1_ffn_in = _L1_ffn_setup()
    _d = {'L0_attn_x': _L0_attn_in['x'], 'L0_attn_time_decay': _L0_attn_in['time_decay'], 'L0_attn_time_first': _L0_attn_in['time_first'], 'L0_attn_time_mix_k': _L0_attn_in['time_mix_k'], 'L0_attn_time_mix_v': _L0_attn_in['time_mix_v'], 'L0_attn_time_mix_r': _L0_attn_in['time_mix_r'], 'L0_attn_Wk': _L0_attn_in['Wk'], 'L0_attn_Wv': _L0_attn_in['Wv'], 'L0_attn_Wr': _L0_attn_in['Wr'], 'L0_attn_Wo': _L0_attn_in['Wo'], 'L0_ffn_router_w': _L0_ffn_in['router_w'], 'L0_ffn_router_b': _L0_ffn_in['router_b'], 'L0_ffn_w1': _L0_ffn_in['w1'], 'L0_ffn_b1': _L0_ffn_in['b1'], 'L0_ffn_w2': _L0_ffn_in['w2'], 'L0_ffn_b2': _L0_ffn_in['b2'], 'L1_attn_gamma': _L1_attn_in['gamma'], 'L1_attn_w_qkv': _L1_attn_in['w_qkv'], 'L1_attn_w_out': _L1_attn_in['w_out'], 'L1_ffn_w_gate': _L1_ffn_in['w_gate'], 'L1_ffn_w_up': _L1_ffn_in['w_up'], 'L1_ffn_w_down': _L1_ffn_in['w_down']}
    _x0 = _d['L0_attn_x']
    _d['L0_attn_x'] = jax.random.normal(jax.random.fold_in(jax.random.key(seed), 1), (1, 2048, 128), dtype=_x0.dtype)
    del _x0
    return _d

def reference(L0_attn_x, L0_attn_time_decay, L0_attn_time_first, L0_attn_time_mix_k, L0_attn_time_mix_v, L0_attn_time_mix_r, L0_attn_Wk, L0_attn_Wv, L0_attn_Wr, L0_attn_Wo, L0_ffn_router_w, L0_ffn_router_b, L0_ffn_w1, L0_ffn_b1, L0_ffn_w2, L0_ffn_b2, L1_attn_gamma, L1_attn_w_qkv, L1_attn_w_out, L1_ffn_w_gate, L1_ffn_w_up, L1_ffn_w_down):

    def _L0_attn_ref(x, time_decay, time_first, time_mix_k, time_mix_v, time_mix_r, Wk, Wv, Wr, Wo):
        import jax, jax.numpy as jnp
        import numpy as np
        B, T, C = (8, 512, 128)

        def _wkv(w_decay, u_first, k, v):
            w = -jnp.exp(w_decay)
            u = u_first
            kt = jnp.transpose(k, (1, 0, 2))
            vt = jnp.transpose(v, (1, 0, 2))
            a0 = jnp.zeros((k.shape[0], k.shape[2]), dtype=k.dtype)
            b0 = jnp.zeros_like(a0)
            p0 = jnp.full_like(a0, -1e+38)

            def step(carry, kv):
                a, b, p = carry
                k_t, v_t = kv
                q = jnp.maximum(p, u + k_t)
                e1 = jnp.exp(p - q)
                e2 = jnp.exp(u + k_t - q)
                y = (e1 * a + e2 * v_t) / (e1 * b + e2)
                q2 = jnp.maximum(p + w, k_t)
                f1 = jnp.exp(p + w - q2)
                f2 = jnp.exp(k_t - q2)
                return ((f1 * a + f2 * v_t, f1 * b + f2, q2), y)
            _, y = jax.lax.scan(step, (a0, b0, p0), (kt, vt))
            return jnp.transpose(y, (1, 0, 2))
        x_prev = jnp.pad(x, ((0, 0), (1, 0), (0, 0)))[:, :-1]
        xk = x_prev + time_mix_k * (x - x_prev)
        xv = x_prev + time_mix_v * (x - x_prev)
        xr = x_prev + time_mix_r * (x - x_prev)
        k = jnp.einsum('btc,dc->btd', xk, Wk)
        v = jnp.einsum('btc,dc->btd', xv, Wv)
        sr = jax.nn.sigmoid(jnp.einsum('btc,dc->btd', xr, Wr))
        wkv = _wkv(time_decay.reshape(-1), time_first.reshape(-1), k, v)
        return jnp.einsum('btc,dc->btd', sr * wkv, Wo)

    def _L0_ffn_ref(x, router_w, router_b, w1, b1, w2, b2):
        import jax, jax.numpy as jnp
        import numpy as np
        NEG_INF = -1e+30

        def _moe_forward(x, router_w, router_b, w1, b1, w2, b2, top_k=2):
            B, S, D = x.shape
            E = router_w.shape[1]
            logits = jnp.einsum('bsd,de->bse', x, router_w) + router_b
            top_vals, top_idx = jax.lax.top_k(logits, top_k)
            keep = jax.nn.one_hot(top_idx, E, dtype=logits.dtype).sum(-2) > 0
            sparse_logits = jnp.where(keep, logits, NEG_INF)
            gating = jax.nn.softmax(sparse_logits, axis=-1)
            xf = x.reshape(-1, D)
            gf = gating.reshape(-1, E)
            h = jax.nn.relu(jnp.einsum('td,edh->eth', xf, w1) + b1[:, None, :])
            y = jnp.einsum('eth,ehd->etd', h, w2) + b2[:, None, :]
            out = jnp.einsum('etd,te->td', y, gf)
            return out.reshape(B, S, D)
        return _moe_forward(x, router_w, router_b, w1, b1, w2, b2, top_k=2)

    def _L1_attn_ref(x, gamma, w_qkv, w_out):
        import jax, jax.numpy as jnp
        import numpy as np
        DIM = 128
        HEADS = 16
        DIM_HEAD = 64
        DIM_INNER = HEADS * DIM_HEAD

        def rms_norm(x, gamma):
            eps = 1e-12
            norm = jnp.maximum(jnp.linalg.norm(x, axis=-1, keepdims=True), eps)
            return x / norm * x.shape[-1] ** 0.5 * (gamma + 1.0)
        b, n, _ = x.shape
        scale = DIM_HEAD ** (-0.5)
        xn = rms_norm(x, gamma)
        qkv = xn @ w_qkv
        qkv = qkv.reshape(b, n, 3, HEADS, DIM_HEAD)
        qkv = jnp.transpose(qkv, (2, 0, 3, 1, 4))
        q, k, v = (qkv[0], qkv[1], qkv[2])
        q = q * scale
        sim = jnp.einsum('bhid,bhjd->bhij', q, k)
        attn = jax.nn.softmax(sim, axis=-1)
        out = jnp.einsum('bhij,bhjd->bhid', attn, v)
        out = jnp.transpose(out, (0, 2, 1, 3)).reshape(b, n, DIM_INNER)
        return out @ w_out

    def _L1_ffn_ref(x, w_gate, w_up, w_down):
        import jax, jax.numpy as jnp
        import numpy as np
        DIM = 128
        HIDDEN = 384
        SCALE = 1.0 / 127.0

        def _dequant(w_int, dtype):
            return w_int.astype(dtype) * jnp.asarray(SCALE, dtype)
        wg = _dequant(w_gate, x.dtype)
        wu = _dequant(w_up, x.dtype)
        wd = _dequant(w_down, x.dtype)
        gate = jnp.einsum('bsd,hd->bsh', x, wg)
        up = jnp.einsum('bsd,hd->bsh', x, wu)
        h = jax.nn.silu(gate) * up
        return jnp.einsum('bsh,dh->bsd', h, wd)
    x = L0_attn_x
    x = x + 0.5 * _L0_ffn_ref(_layernorm(x, axis=-1), L0_ffn_router_w, L0_ffn_router_b, L0_ffn_w1, L0_ffn_b1, L0_ffn_w2, L0_ffn_b2)
    x = x + _L0_attn_ref(_layernorm(x, axis=-1), L0_attn_time_decay, L0_attn_time_first, L0_attn_time_mix_k, L0_attn_time_mix_v, L0_attn_time_mix_r, L0_attn_Wk, L0_attn_Wv, L0_attn_Wr, L0_attn_Wo)
    x = x + 0.5 * _L0_ffn_ref(_layernorm(x, axis=-1), L0_ffn_router_w, L0_ffn_router_b, L0_ffn_w1, L0_ffn_b1, L0_ffn_w2, L0_ffn_b2)
    x = x + 0.5 * _L1_ffn_ref(_layernorm(x, axis=-1), L1_ffn_w_gate, L1_ffn_w_up, L1_ffn_w_down)
    x = x + _L1_attn_ref(_layernorm(x, axis=-1), L1_attn_gamma, L1_attn_w_qkv, L1_attn_w_out)
    x = x + 0.5 * _L1_ffn_ref(_layernorm(x, axis=-1), L1_ffn_w_gate, L1_ffn_w_up, L1_ffn_w_down)
    return x

_drawn_inputs = setup_inputs


def setup_inputs(seed=0):
    import zlib

    import numpy as np

    out = dict(_drawn_inputs(seed))
    spreads = {'L0_ffn_router_b': (0.0, 0.1),
     'L0_ffn_b1': (0.0, 0.1),
     'L0_ffn_b2': (0.0, 0.1),
     'L1_attn_gamma': (0.0, 0.8)}
    factors = {'L1_attn_w_qkv': 8.0, 'L1_attn_w_out': 8.0}
    for name, (base, spread) in spreads.items():
        noise = np.random.default_rng([zlib.crc32(name.encode()), seed]).standard_normal(out[name].shape)
        drawn = base * np.exp(spread * noise) if base else spread * noise
        out[name] = jnp.asarray(drawn.astype(out[name].dtype))
    for name, factor in factors.items():
        out[name] = (out[name] * factor).astype(out[name].dtype)
    return out
```

```python
import concourse.bass as bass
from concourse import mybir
from concourse.alu_op_type import AluOpType as ALU
from contextlib import ExitStack

fp32 = mybir.dt.float32
fp32r = mybir.dt.float32r
int32 = mybir.dt.int32
ACT = mybir.ActivationFunctionType
AX = mybir.AxisListType
ds = bass.ds

C = 128
T = 2048
CH = 512
NC = T // CH
NT = T // 128
TPC = CH // 128
E, H0 = 8, 512
HT0 = H0 // 128
UNITS = E * HT0
HEADS, DH = 16, 64
PAIRS = HEADS // 2
H1 = 384
HT1 = H1 // 128
GROUPS = NT // 2
LN_EPS = 1e-5
RMS_EPS = 1e-12
QUANT_SCALE = 1.0 / 127.0
SCORE_SCALE = DH ** -0.5
NO_STATE = -1e38
EXCLUDE = -3.0e38
LAG = 3
PRIME = 1
WKV_SLOTS = (1, 2, 4, 3)


def macaron_kernel(nc, a, out, l_scratch, r_scratch):
    ctx = ExitStack()
    with ctx:
        def sb(name, shape, dt=fp32, where=ctx):
            return where.enter_context(nc.sbuf_tensor(name, shape, dt))

        def sem(name):
            return ctx.enter_context(nc.semaphore(name))

        x = sb("x", [C, T])
        xnp = sb("xnp", [C, T + 1])
        xn = xnp[:, 1:T + 1]
        xprev = xnp[:, 0:T]
        big = sb("big", [C, PAIRS, T + 8])
        ident = sb("ident", [128, 128])
        inv_c = sb("inv_c", [128, 128])
        ln_v = sb("ln_v", [128, NT])
        ln_s = sb("ln_s", [128, NT])
        ln_r = sb("ln_r", [128, NT])
        wgu_i = sb("wgu_i", [C, 2, H1], int32)
        wd_i = sb("wd_i", [128, HT1, C], int32)
        wgu = sb("wgu", [C, 2, H1])
        wd = sb("wd", [128, HT1, C])
        w_out = sb("w_out", [128, PAIRS, C])
        gamma1 = sb("gamma1", [C, 1])
        cen = big[:, 0, 0:T]
        sqr = big[:, 1, 0:T]
        f_sig = big[:, 2, 0:HT1 * CH].rearrange("p (a n) -> p a n", a=HT1)
        f_h = big[:, 3, 0:HT1 * CH].rearrange("p (a n) -> p a n", a=HT1)

        one = ExitStack()
        w1 = sb("w1", [C, E, H0], where=one)
        w2 = sb("w2", [128, E, HT0, C], where=one)
        b1 = sb("b1", [128, E, HT0], where=one)
        b2 = sb("b2", [E, C], where=one)
        rw = sb("rw", [C, E], where=one)
        rb = sb("rb", [128, E], where=one)
        rank = sb("rank", [128, E], where=one)
        lg = sb("lg", [128, NT, E], where=one)
        lg2 = sb("lg2", [128, NT, E], where=one)
        eq = sb("eq", [128, NT, E], where=one)
        best = sb("best", [128, NT, E], where=one)
        second = sb("second", [128, NT, E], where=one)
        gates = sb("gates", [128, NT, E], where=one)
        rt = sb("rt", [128, 8, NT], where=one)
        g_t = sb("g_t", [E, T], where=one)
        sel = sb("sel", [E, E, 128], where=one)
        h_raw = sb("h_raw", [128, 4, CH], where=one)
        h_gated = sb("h_gated", [128, 4, CH], where=one)
        rwkv_w = sb("rwkv_w", [C, 4, C], where=one)
        mix = sb("mix", [C, 5], where=one)
        decay = sb("decay", [C, 2], where=one)
        one.close()

        two = ExitStack()
        ka = [sb(f"ka{i}", [128, T], fp32r, two) for i in range(2)]
        kb = [sb(f"kb{i}", [DH + 1, T], fp32r, two) for i in range(2)]
        qa = [sb(f"qa{i}", [128, T], fp32r, two) for i in range(2)]
        qb = [sb(f"qb{i}", [DH + 1, T], fp32r, two) for i in range(2)]
        v_even = sb("v_even", [128, NT, DH + 1], where=two)
        v_odd = sb("v_odd", [128, NT, 128], where=two)
        probs = sb("probs", [128, 2, 2, CH], where=two)
        w_qk = [sb(f"w_qk{i}", [C, 2, 2, DH], where=two) for i in range(2)]
        w_v = sb("w_v", [C, 2 * DH], where=two)
        m_part = sb("m_part", [128, NC, NT], where=two)
        m_col = [sb(f"m_col{i}", [128, NT], where=two) for i in range(2)]
        l_row = sb("l_row", [DH + 1, T], where=two)
        l_col = sb("l_col", [128, 2, NT], where=two)
        r_col = sb("r_col", [128, 2, NT], where=two)
        r_bc = sb("r_bc", [128, T], where=two)
        two.close()

        ps = ctx.enter_context(nc.psum_tensor("ps", [128, 8, CH], fp32))

        x_loaded = sem("x_loaded")
        small_loaded = sem("small_loaded")
        w1_loaded, w2_loaded = sem("w1_loaded"), sem("w2_loaded")
        l1_loaded = sem("l1_loaded")
        const_step, const_ready = sem("const_step"), sem("const_ready")
        l1_const = sem("l1_const")
        dequantised = sem("dequantised")
        x_ready = sem("x_ready")
        dve_step = sem("dve_step")
        act_step = sem("act_step")
        ln_mean, ln_cen, ln_sq, ln_var = sem("ln_mean"), sem("ln_cen"), sem("ln_sq"), sem("ln_var")
        ln_add, ln_std, ln_rec, ln_bc, ln_out = sem("ln_add"), sem("ln_std"), sem("ln_rec"), sem("ln_bc"), sem("ln_out")
        rt_logits, rt_diff, rt_exp, rt_gates = sem("rt_logits"), sem("rt_diff"), sem("rt_exp"), sem("rt_gates")
        gt_ps, gt_done = sem("gt_ps"), sem("gt_done")
        h_ps, h_relu, g_ps, h_done = sem("h_ps"), sem("h_relu"), sem("g_ps"), sem("h_done")
        w2_done, y_ps = sem("w2_done"), sem("y_ps")
        mixed, kvr_ps, kvr_done, wkv_arg, wkv_exp = sem("mixed"), sem("kvr_ps"), sem("kvr_done"), sem("wkv_arg"), sem("wkv_exp")
        wkv_out, o_ps = sem("wkv_out"), sem("o_ps")
        f_ps, f_sigmoid, f_hid, f_down = sem("f_ps"), sem("f_sigmoid"), sem("f_hid"), sem("f_down")
        f_silu = sem("f_silu")
        rms_sq, rms_sum, rms_add, rms_std, rms_rec, rms_bc, rms_out = (
            sem("rms_sq"), sem("rms_sum"), sem("rms_add"), sem("rms_std"), sem("rms_rec"), sem("rms_bc"), sem("rms_out"))
        wqk_loaded = [sem("wqk_loaded0"), sem("wqk_loaded1")]
        wv_loaded = sem("wv_loaded")
        v_ps, v_done = sem("v_ps"), sem("v_done")
        proj_ps, hi_done, lo_done, kb_done = sem("proj_ps"), sem("hi_done"), sem("lo_done"), sem("kb_done")
        m_ps, m_done, m_ready = sem("m_ps"), sem("m_done"), sem("m_ready")
        st_ps, exp_done, pv_done = sem("st_ps"), sem("exp_done"), sem("pv_done")
        s_ps, s_max = sem("s_ps"), sem("s_max")
        o_done, l_done = sem("o_done"), sem("l_done")
        l_stored, l_loaded, r_ready, r_stored, r_loaded, o_scaled = (
            sem("l_stored"), sem("l_loaded"), sem("r_ready"), sem("r_stored"), sem("r_loaded"), sem("o_scaled"))
        out_ps = sem("out_ps")
        stored = sem("stored")

        block = ctx.enter_context(nc.Block())

        def chunk(c):
            return ds(c * CH, CH)

        def wait_x(eng, k):
            if k == 0:
                eng.wait_ge(x_loaded, 16)
            else:
                eng.wait_ge(x_ready, PRIME + NC * k)

        @block.sync
        def _(sp):
            sp.dma_start(x[:, :], a["xT"]).then_inc(x_loaded, 16)
            sp.dma_start(rw[:, :], a["router_w"]).then_inc(small_loaded, 16)
            sp.dma_start(rb[:, :], a["router_b"].rearrange("(a e) -> a e", a=1).to_broadcast([128, E])).then_inc(small_loaded, 16)
            sp.dma_start(b1[:, :, :], a["b1T"]).then_inc(small_loaded, 16)
            sp.dma_start(b2[:, :], a["b2"]).then_inc(small_loaded, 16)
            sp.dma_start(w1[:, :, :], a["w1T"]).then_inc(w1_loaded, 16)
            sp.dma_start(w2[:, :, :, :], a["w2T"]).then_inc(w2_loaded, 16)
            sp.dma_start(rwkv_w[:, :, :], a["rwkv_wT"]).then_inc(small_loaded, 16)
            sp.dma_start(mix[:, :], a["mix"]).then_inc(small_loaded, 16)
            sp.dma_start(wgu_i[:, :, :], a["w_gate_upT"]).then_inc(l1_loaded, 16)
            sp.dma_start(wd_i[:, :, :], a["w_downT"]).then_inc(l1_loaded, 16)
            sp.dma_start(w_out[:, :, :], a["w_outT"]).then_inc(l1_loaded, 16)
            sp.dma_start(gamma1[:, :], a["gamma"]).then_inc(l1_loaded, 16)

            def normalise(pair, par):
                head = 2 * pair + par
                row = DH if par == 0 else 0
                sp.wait_ge(l_done, PRIME + NC * (head + 1))
                sp.dma_start(l_scratch[ds(head, 1), :], l_row[row:row + 1, :]).then_inc(l_stored, 16)
                sp.wait_ge(l_stored, 16 * (head + 1))
                sp.dma_start(l_col[:, par, :], l_scratch[ds(head, 1), :].rearrange("a (p t) -> (a p) t", p=128)).then_inc(l_loaded, 16)
                sp.wait_ge(r_ready, head + 1)
                sp.dma_start(r_scratch[ds(head, 1), :].rearrange("a (p t) -> (a p) t", p=128), r_col[:, par, :]).then_inc(r_stored, 16)
                sp.wait_ge(r_stored, 16 * (head + 1))
                sp.wait_ge(o_scaled, PRIME + head)
                sp.dma_start(r_bc[par * DH:par * DH + DH, :],
                             r_scratch[ds(head, 1), :].to_broadcast([DH, T])).then_inc(r_loaded, 16)
            with sp.Fori(0, PAIRS) as pair:
                normalise(pair, 0)
                normalise(pair, 1)
            for c in range(NC):
                sp.wait_ge(x_ready, PRIME + NC * 5 + c + 1)
                sp.dma_start(out[:, chunk(c)], x[:, chunk(c)]).then_inc(stored, 16)
            sp.wait_ge(stored, 16 * NC)

        @block.gpsimd
        def _(pool):
            nc.gpsimd.memset(ident[:, :], 0.0).then_inc(const_step, 1)
            nc.gpsimd.memset(sel[:, :, :], 0.0).then_inc(const_step, 1)
            nc.gpsimd.memset(inv_c[:, :], 1.0 / C).then_inc(const_ready, 1)
            nc.gpsimd.memset(xnp[:, 0:1], 0.0).then_inc(const_ready, 1)
            for e in range(E):
                nc.gpsimd.memset(rank[:, e:e + 1], float(E - e)).then_inc(const_ready, 1)
            pool.wait_ge(const_step, 2)
            nc.gpsimd.affine_select(out=ident[:, :], in_=ident[:, :], compare_op=ALU.not_equal, fill=1.0,
                                    base=0, pattern=[[-1, 128]], channel_multiplier=1).then_inc(const_ready, 1)
            nc.gpsimd.affine_select(out=sel[:, :, :], in_=sel[:, :, :], compare_op=ALU.not_equal, fill=1.0,
                                    base=0, pattern=[[-1, E], [0, 128]], channel_multiplier=1).then_inc(const_ready, 1)
            pool.wait_ge(x_ready, PRIME + NC * 4)
            for i in range(2):
                nc.gpsimd.memset(kb[i][DH:DH + 1, :].bitcast(fp32), 1.0).then_inc(l1_const, 1)
            pool.wait_ge(l1_const, 2)
            nc.gpsimd.memset(v_even[:, :, DH:DH + 1], 1.0).then_inc(l1_const, 1)
            nc.gpsimd.memset(v_odd[:, :, 0:1], 1.0).then_inc(l1_const, 1)
            nc.gpsimd.memset(v_odd[:, :, 1:DH], 0.0).then_inc(l1_const, 1)

            def scale_head(pair, par):
                head = 2 * pair + par
                rows = slice(par * DH, par * DH + DH)
                pool.wait_ge(r_loaded, 16 * (head + 1))
                pool.wait_ge(o_done, PRIME + NC * (head + 1))
                o = big[rows, ds(pair, 1), 0:T].rearrange("p a t -> p (a t)")
                nc.gpsimd.tensor_tensor(o, o, r_bc[rows, :], ALU.mult).then_inc(o_scaled, 1)
            with pool.Fori(0, PAIRS) as pair:
                scale_head(pair, 0)
                scale_head(pair, 1)
        CONST = 2 + E + 2
        L1_CONST = 5

        @block.tensor
        def _(pe):
            mm = nc.tensor.matmul

            def layer_norm(k):
                wait_x(pe, k)
                if k == 0:
                    pe.wait_ge(const_ready, CONST)
                for c in range(NC):
                    mm(ps[:, c, :], inv_c[:, :], x[:, chunk(c)], start=True, stop=True).then_inc(ln_mean, 1)
                for c in range(NC):
                    pe.wait_ge(ln_sq, NC * k + c + 1)
                    for t in range(TPC * c, TPC * c + TPC):
                        last = mm(ps[:, 4, t:t + 1], sqr[:, t * 128:t * 128 + 128], inv_c[:, 0:1], start=True, stop=True)
                last.then_inc(ln_var, 1)
                pe.wait_ge(ln_rec, k + 1)
                for c in range(NC):
                    for t in range(TPC):
                        last = mm(ps[:, c, t * 128:t * 128 + 128],
                                  ln_r[:, TPC * c + t:TPC * c + t + 1].to_broadcast([128, 128]), ident[:, :], start=True, stop=True)
                    last.then_inc(ln_bc, 1)

            def moe(k):
                pe.wait_ge(ln_out, NC * (k * 2 + 1))
                pe.wait_ge(small_loaded, 16 * 6)
                for t in range(NT):
                    last = mm(ps[:, 5, t * E:t * E + E], xn[:, t * 128:t * 128 + 128], rw[:, :], start=True, stop=True)
                last.then_inc(rt_logits, 1)
                pe.wait_ge(rt_gates, k + 1)
                for c in range(NC):
                    for t in range(TPC):
                        last = mm(ps[0:E, c, t * 128:t * 128 + 128], gates[:, TPC * c + t, :], ident[:, :], start=True, stop=True)
                    last.then_inc(gt_ps, 1)
                pe.wait_ge(gt_done, NC * (k + 1))
                if k == 0:
                    pe.wait_ge(w1_loaded, 16)
                    pe.wait_ge(w2_loaded, 16)
                with pe.Fori(0, NC) as c:
                    at = (k * NC + c)
                    def second_product(u):
                        e, ht = u // HT0, u % HT0
                        pe.wait_ge(h_done, PRIME + at * UNITS + u + 1)
                        m = mm(ps[:, 6, :], w2[:, e, ht, :], h_gated[:, u % 4, :], start=False, stop=(u == UNITS - 1))
                        m.then_inc(w2_done, 1)
                        return m
                    for u in range(UNITS):
                        e, ht = u // HT0, u % HT0
                        if u == 0:
                            pe.wait_ge(x_ready, PRIME + (NC * 2 * k) + c)
                        if ht == 0:
                            pe.wait_ge(h_done, PRIME + at * UNITS + max(u - HT0, 0))
                        pe.wait_ge(h_relu, PRIME + at * UNITS + max(u - 3, 0))
                        mm(ps[:, u % 4, :], w1[:, e, ht * 128:ht * 128 + 128], xnp[:, ds(c * CH + 1, CH)],
                           start=True, stop=True).then_inc(h_ps, 1)
                        if ht == 0:
                            mm(ps[:, 4 + e % 2, :], sel[:, e, :], g_t[:, chunk(c)], start=True, stop=True).then_inc(g_ps, 1)
                        if u == 0:
                            mm(ps[:, 6, :], b2[:, :], g_t[:, chunk(c)], start=True, stop=False)
                        if u >= LAG:
                            second_product(u - LAG)
                    for u in range(UNITS - LAG, UNITS):
                        last = second_product(u)

            def rwkv():
                for j in range(3):
                    pe.wait_ge(mixed, j + 1)
                    for c in range(NC):
                        if j == 2:
                            pe.wait_ge(kvr_done, c + 1)
                        mm(ps[:, (4 if j == 1 else 0) + c, :], rwkv_w[:, j, :], big[:, 2 + j, ds(c * CH, CH)],
                           start=True, stop=True).then_inc(kvr_ps, 1)
                pe.wait_ge(wkv_out, 1)
                for c in range(NC):
                    mm(ps[:, 4 + c, :], rwkv_w[:, 3, :], big[:, 2, ds(c * CH, CH)], start=True, stop=True).then_inc(o_ps, 1)

            def quant_ffn(k, before):
                pe.wait_ge(ln_out, NC * (before + 1))
                pe.wait_ge(dequantised, 2)
                with pe.Fori(0, NC) as c:
                    at = k * NC + c
                    for ht in range(HT1):
                        if ht == 0:
                            pe.wait_ge(f_hid, PRIME + at * HT1)
                        for g in range(2):
                            last = mm(ps[:, 2 * ht + g, :], wgu[:, g, ht * 128:ht * 128 + 128],
                                      xnp[:, ds(c * CH + 1, CH)], start=True, stop=True)
                        last.then_inc(f_ps, 1)
                    pe.wait_ge(x_ready, PRIME + NC * before + c)
                    for ht in range(HT1):
                        pe.wait_ge(f_hid, PRIME + at * HT1 + ht + 1)
                        last = mm(ps[:, 6, :], wd[:, ht, :], f_h[:, ht, :], start=(ht == 0), stop=(ht == HT1 - 1))
                    last.then_inc(f_down, 1)

            def rms_norm():
                for c in range(NC):
                    pe.wait_ge(rms_sq, c + 1)
                    for t in range(TPC * c, TPC * c + TPC):
                        last = mm(ps[:, 4, t:t + 1], sqr[:, t * 128:t * 128 + 128], inv_c[:, 0:1], start=True, stop=True)
                last.then_inc(rms_sum, 1)
                pe.wait_ge(rms_rec, 1)
                for c in range(NC):
                    for t in range(TPC):
                        last = mm(ps[:, c, t * 128:t * 128 + 128],
                                  ln_r[:, TPC * c + t:TPC * c + t + 1].to_broadcast([128, 128]), ident[:, :], start=True, stop=True)
                    last.then_inc(rms_bc, 1)

            def project_qk(head, par, turn):
                pe.wait_ge(wqk_loaded[par], 64 * turn)
                for c in range(NC):
                    for s in range(2):
                        if c < 2:
                            pe.wait_ge(s_max, PRIME + NC * NT * head)
                            if not (isinstance(head, int) and head == 0):
                                pe.wait_ge(o_done, PRIME + NC * (head - 1))
                                pe.wait_ge(l_done, PRIME + NC * (head - 1))
                        else:
                            pe.wait_ge(lo_done, 8 * head + 2 * (c - 2) + s + 1)
                        mm(ps[:, 4 + 2 * (c % 2) + s, :], w_qk[par][:, s, :, :].rearrange("p a d -> p (a d)"),
                           xn[:, c * CH:c * CH + CH], start=True, stop=True).then_inc(proj_ps, 1)

            def project_v(pair):
                pe.wait_ge(wv_loaded, 16 * (pair + 1))
                for t in range(NT):
                    last = mm(ps[:, t // 4, (t % 4) * 128:(t % 4) * 128 + 128], xn[:, t * 128:t * 128 + 128], w_v[:, :],
                              start=True, stop=True)
                    if t % 4 == 3:
                        last.then_inc(v_ps, 1)

            def score_tile(head, par, c, it):
                if it < 2:
                    pe.wait_ge(s_max, PRIME + NC * NT * head + NT * c)
                else:
                    pe.wait_ge(s_max, PRIME + NC * NT * head + NT * c + it - 1)
                mm(ps[:, 4 + it % 2, :], qa[par][:, it * 128:it * 128 + 128], ka[par][:, ds(c * CH, CH)],
                   start=True, stop=True).then_inc(s_ps, 1)

            def maxima_row(head, par):
                pe.wait_ge(m_ready, head + 1)
                for t in range(NT):
                    last = mm(ps[DH:DH + 1, t // 4, (t % 4) * 128:(t % 4) * 128 + 128], m_col[par][:, t:t + 1], ident[:, :],
                              start=True, stop=True)
                    if t % 4 == 3:
                        last.then_inc(m_ps, 1)

            def values(head, par, c, g):
                pe.wait_ge(exp_done, GROUPS * NC * head + GROUPS * c + g + 1)
                if g == 0:
                    pe.wait_ge(o_done, PRIME + NC * head + c)
                    pe.wait_ge(l_done, PRIME + NC * head + c)
                for j in range(2):
                    jt = 2 * g + j
                    v = v_even[:, jt, :] if par == 0 else v_odd[:, jt, :]
                    o = ps[0:DH + 1, 6, :] if par == 0 else ps[:, 6, :]
                    last = mm(o, v, probs[:, g % 2, j, :], start=(jt == 0), stop=(jt == NT - 1))
                last.then_inc(pv_done, 1)

            def scores_t(head, par, c, g):
                for j in range(2):
                    jt = 2 * g + j
                    st = ps[:, 2 * (g % 2) + j, :]
                    mm(st, ka[par][:, jt * 128:jt * 128 + 128], qa[par][:, ds(c * CH, CH)], start=True, stop=False)
                    last = mm(st, kb[par][:, jt * 128:jt * 128 + 128], qb[par][:, ds(c * CH, CH)], start=False, stop=True)
                last.then_inc(st_ps, 1)

            def main_chunk(head, par, c, first, with_next):
                n0 = GROUPS * NC * head + GROUPS * c
                for g in range(GROUPS):
                    if not first or g >= 2:
                        pe.wait_ge(exp_done, n0 + g - 1)
                    scores_t(head, par, c, g)
                    if g == 0 and not first:
                        values(head, par, c - 1, GROUPS - 1)
                    if with_next:
                        for it in (2 * g, 2 * g + 1):
                            score_tile(head + 1, 1 - par, c, it)
                    if g >= 1:
                        values(head, par, c, g - 1)

            def window(pair, par, with_next):
                head = 2 * pair + par
                if par == 0:
                    project_v(pair)
                if with_next:
                    project_qk(head + 1, 1 - par, pair + 1 + par)
                if par == 0:
                    pe.wait_ge(v_done, 8 * (pair + 1))
                maxima_row(head, par)
                pe.wait_ge(kb_done, NC * (head + 1))
                pe.wait_ge(m_done, NC * (head + 1))
                if with_next:
                    pe.wait_ge(lo_done, 8 * (head + 2))
                main_chunk(head, par, 0, True, with_next)
                with pe.Fori(1, NC) as c:
                    main_chunk(head, par, c, False, with_next)
                values(head, par, NC - 1, GROUPS - 1)

            def attention():
                pe.wait_ge(rms_out, NC)
                pe.wait_ge(l1_const, L1_CONST)
                project_qk(0, 0, 1)
                pe.wait_ge(lo_done, 8)
                with pe.Fori(0, NC) as c:
                    for it in range(NT):
                        score_tile(0, 0, c, it)
                with pe.Fori(0, PAIRS - 1) as pair:
                    window(pair, 0, True)
                    window(pair, 1, True)
                window(PAIRS - 1, 0, True)
                window(PAIRS - 1, 1, False)
                pe.wait_ge(o_scaled, PRIME + HEADS)
                for c in range(NC):
                    for p in range(PAIRS):
                        last = mm(ps[:, c, :], w_out[:, p, :], big[:, p, c * CH:c * CH + CH],
                                  start=(p == 0), stop=(p == PAIRS - 1))
                    last.then_inc(out_ps, 1)

            layer_norm(0)
            moe(0)
            layer_norm(1)
            rwkv()
            layer_norm(2)
            moe(1)
            layer_norm(3)
            quant_ffn(0, 3)
            layer_norm(4)
            rms_norm()
            attention()
            layer_norm(5)
            quant_ffn(1, 5)

        @block.scalar
        def _(act):
            af = nc.scalar.activation

            def layer_norm(k):
                for c in range(NC):
                    act.wait_ge(ln_cen, NC * k + c + 1)
                    af(sqr[:, chunk(c)], cen[:, chunk(c)], ACT.Square).then_inc(ln_sq, 1)
                act.wait_ge(ln_add, k + 1)
                af(ln_s[:, :], ln_v[:, :], ACT.Sqrt).then_inc(ln_std, 1)

            def moe(k):
                act.wait_ge(rt_diff, k + 1)
                af(rt[:, 3, :], rt[:, 2, :], ACT.Exp).then_inc(rt_exp, 1)
                for c in range(NC):
                    act.wait_ge(gt_ps, NC * k + c + 1)
                    af(g_t[:, chunk(c)], ps[0:E, c, :], ACT.Copy).then_inc(gt_done, 1)
                with act.Fori(0, NC) as c:
                    at = k * NC + c
                    for u in range(UNITS):
                        e, ht = u // HT0, u % HT0
                        act.wait_ge(h_ps, at * UNITS + u + 1)
                        act.wait_ge(h_done, PRIME + at * UNITS + max(u - 3, 0))
                        af(h_raw[:, u % 4, :], ps[:, u % 4, :], ACT.Relu, bias=b1[:, e, ht:ht + 1]).then_inc(h_relu, 1)

            def rwkv():
                act.wait_ge(small_loaded, 16 * 6)
                af(decay[:, 0:1], mix[:, 3:4], ACT.Exp).then_inc(act_step, 1)
                for j in range(3):
                    for c in range(NC):
                        act.wait_ge(kvr_ps, NC * j + c + 1)
                        src = ps[:, (4 if j == 1 else 0) + c, :]
                        af(big[:, 5 + j, ds(c * CH, CH)], src, ACT.Copy if j < 2 else ACT.Sigmoid).then_inc(kvr_done, 1)
                for n in range(4):
                    act.wait_ge(wkv_arg, n + 1)
                    s = WKV_SLOTS[n]
                    af(big[:, s, 1:T + 1], big[:, s, 1:T + 1], ACT.Exp).then_inc(wkv_exp, 1)

            def quant_ffn(k):
                with act.Fori(0, NC) as c:
                    at = k * NC + c
                    for ht in range(HT1):
                        act.wait_ge(f_ps, at * HT1 + ht + 1)
                        af(f_sig[:, ht, :], ps[:, 2 * ht, :], ACT.Sigmoid).then_inc(f_sigmoid, 1)

            def rms_norm():
                for c in range(NC):
                    act.wait_ge(ln_out, NC * 4 + c + 1)
                    af(sqr[:, chunk(c)], xn[:, chunk(c)], ACT.Square).then_inc(rms_sq, 1)
                act.wait_ge(rms_add, 1)
                af(ln_s[:, :], ln_v[:, :], ACT.Sqrt).then_inc(rms_std, 1)

            def load_qk(head, par):
                for s in range(2):
                    for dup in range(2):
                        act.dma_start(w_qk[par][:, s, dup, :],
                                     a["w_qkv"][:, ds(head * DH + s * HEADS * DH, DH)]).then_inc(wqk_loaded[par], 16)

            def load_v(pair):
                act.dma_start(w_v[:, :], a["w_qkv"][:, ds(pair * 2 * DH + 2 * HEADS * DH, 2 * DH)]).then_inc(wv_loaded, 16)

            def evacuate_qk(head, par):
                for c in range(NC):
                    for s in range(2):
                        act.wait_ge(proj_ps, 8 * head + 2 * c + s + 1)
                        dst = (qa if s == 0 else ka)[par]
                        af(dst[:, c * CH:c * CH + CH], ps[:, 4 + 2 * (c % 2) + s, :], ACT.Copy,
                           scale=SCORE_SCALE if s == 0 else 1.0).then_inc(hi_done, 1)

            def evacuate_v(pair):
                for b in range(4):
                    act.wait_ge(v_ps, 4 * pair + b + 1)
                    src = ps[:, b, :].rearrange("p (t d) -> p t d", t=4)
                    af(v_even[:, 4 * b:4 * b + 4, 0:DH], src[:, :, 0:DH], ACT.Copy).then_inc(v_done, 1)
                    af(v_odd[:, 4 * b:4 * b + 4, DH:128], src[:, :, DH:128], ACT.Copy).then_inc(v_done, 1)

            def maxima_row(head, par):
                for b in range(NC):
                    act.wait_ge(m_ps, NC * head + b + 1)
                    af(qb[par][DH:DH + 1, b * CH:b * CH + CH], ps[DH:DH + 1, b, :], ACT.Copy).then_inc(m_done, 1)

            def row_sums(head, par, c):
                row = DH if par == 0 else 0
                act.wait_ge(pv_done, GROUPS * (NC * head + c + 1))
                af(l_row[row:row + 1, ds(c * CH, CH)], ps[row:row + 1, 6, :], ACT.Copy).then_inc(l_done, 1)

            def main_chunk(head, par, c, first):
                n0 = GROUPS * NC * head + GROUPS * c
                for g in range(GROUPS):
                    act.wait_ge(st_ps, n0 + g + 1)
                    if not first or g >= 2:
                        act.wait_ge(pv_done, n0 + g - 1)
                    af(probs[:, g % 2, :, :], ps[:, 2 * (g % 2):2 * (g % 2) + 2, :], ACT.Exp).then_inc(exp_done, 1)
                    if g == 0 and not first:
                        row_sums(head, par, c - 1)

            def window(pair, par, with_next, load):
                head = 2 * pair + par
                if par == 0:
                    evacuate_v(pair)
                if with_next:
                    evacuate_qk(head + 1, 1 - par)
                if load:
                    load_qk(head + 2, par)
                    if par == 0:
                        load_v(pair + 1)
                maxima_row(head, par)
                main_chunk(head, par, 0, True)
                if par == 1:
                    act.wait_ge(l_stored, 16 * head)
                with act.Fori(1, NC) as c:
                    main_chunk(head, par, c, False)
                row_sums(head, par, NC - 1)

            def attention():
                act.wait_ge(x_ready, PRIME + NC * 4)
                load_qk(0, 0)
                load_v(0)
                load_qk(1, 1)
                evacuate_qk(0, 0)
                with act.Fori(0, PAIRS - 1) as pair:
                    window(pair, 0, True, True)
                    window(pair, 1, True, True)
                window(PAIRS - 1, 0, True, False)
                window(PAIRS - 1, 1, False, False)

            layer_norm(0)
            moe(0)
            layer_norm(1)
            rwkv()
            layer_norm(2)
            moe(1)
            layer_norm(3)
            quant_ffn(0)
            layer_norm(4)
            rms_norm()
            attention()
            layer_norm(5)
            quant_ffn(1)

        @block.vector
        def _(dve):
            tt = nc.vector.tensor_tensor
            stt = nc.vector.scalar_tensor_tensor
            ts = nc.vector.tensor_scalar
            for primed in (x_ready, h_done, h_relu, w2_done, s_max, o_scaled, f_hid, f_down, o_done, l_done):
                nc.vector.sem_inc(primed, PRIME)
            steps = [0]

            def step(ins):
                steps[0] += 1
                ins.then_inc(dve_step, 1)
                dve.wait_ge(dve_step, steps[0])

            def layer_norm(k):
                for c in range(NC):
                    dve.wait_ge(ln_mean, NC * k + c + 1)
                    tt(cen[:, chunk(c)], x[:, chunk(c)], ps[:, c, :], ALU.subtract).then_inc(ln_cen, 1)
                dve.wait_ge(ln_var, k + 1)
                ts(ln_v[:, :], ps[:, 4, 0:NT], LN_EPS, None, ALU.add).then_inc(ln_add, 1)
                dve.wait_ge(ln_std, k + 1)
                nc.vector.reciprocal(ln_r[:, :], ln_s[:, :]).then_inc(ln_rec, 1)
                for c in range(NC):
                    dve.wait_ge(ln_bc, NC * k + c + 1)
                    dve.wait_ge(ln_cen, NC * (k + 1))
                    tt(xn[:, chunk(c)], cen[:, chunk(c)], ps[:, c, :], ALU.mult).then_inc(ln_out, 1)

            def bc(col):
                return col.rearrange("p (t a) -> p t a", a=1).to_broadcast([128, NT, E])

            def pick(src, hot, top):
                step(nc.vector.tensor_reduce(rt[:, top, :], src[:, :, :], AX.X, ALU.max))
                step(tt(eq[:, :, :], src[:, :, :], bc(rt[:, top, :]), ALU.is_equal))
                step(tt(eq[:, :, :], eq[:, :, :],
                        rank[:, :].rearrange("p (a e) -> p a e", a=1).to_broadcast([128, NT, E]), ALU.mult))
                step(nc.vector.tensor_reduce(rt[:, 7, :], eq[:, :, :], AX.X, ALU.max))
                step(tt(hot[:, :, :], eq[:, :, :], bc(rt[:, 7, :]), ALU.is_equal))

            def moe(k):
                if k == 0:
                    dve.wait_ge(const_ready, CONST)
                    dve.wait_ge(small_loaded, 16 * 6)
                dve.wait_ge(rt_logits, k + 1)
                step(tt(lg[:, :, :], ps[:, 5, 0:NT * E].rearrange("p (t e) -> p t e", e=E),
                        rb[:, :].rearrange("p (a e) -> p a e", a=1).to_broadcast([128, NT, E]), ALU.add))
                pick(lg, best, 0)
                step(stt(lg2[:, :, :], best[:, :, :], EXCLUDE, lg[:, :, :], ALU.mult, ALU.add))
                pick(lg2, second, 1)
                tt(rt[:, 2, :], rt[:, 1, :], rt[:, 0, :], ALU.subtract).then_inc(rt_diff, 1)
                dve.wait_ge(rt_exp, k + 1)
                step(ts(rt[:, 4, :], rt[:, 3, :], 1.0, None, ALU.add))
                step(nc.vector.reciprocal(rt[:, 5, :], rt[:, 4, :]))
                step(tt(rt[:, 6, :], rt[:, 3, :], rt[:, 5, :], ALU.mult))
                step(tt(best[:, :, :], best[:, :, :], bc(rt[:, 5, :]), ALU.mult))
                step(tt(second[:, :, :], second[:, :, :], bc(rt[:, 6, :]), ALU.mult))
                tt(gates[:, :, :], best[:, :, :], second[:, :, :], ALU.add).then_inc(rt_gates, 1)
                with dve.Fori(0, NC) as c:
                    at = k * NC + c
                    for u in range(UNITS):
                        e, ht = u // HT0, u % HT0
                        if ht == 0:
                            dve.wait_ge(g_ps, at * E + e + 1)
                        dve.wait_ge(h_relu, PRIME + at * UNITS + u + 1)
                        dve.wait_ge(w2_done, PRIME + at * UNITS + max(u - 3, 0))
                        tt(h_gated[:, u % 4, :], h_raw[:, u % 4, :], ps[:, 4 + e % 2, :], ALU.mult).then_inc(h_done, 1)
                    dve.wait_ge(w2_done, PRIME + at * UNITS + UNITS)
                    stt(x[:, ds(c * CH, CH)], ps[:, 6, :], 0.5, x[:, ds(c * CH, CH)], ALU.mult, ALU.add).then_inc(x_ready, 1)

            def rwkv():
                s = lambda n, off=0: big[:, n, off:off + T]
                dve.wait_ge(ln_out, NC * 2)
                step(tt(s(0), xn, xprev, ALU.subtract))
                for j in range(3):
                    stt(s(2 + j), s(0), mix[:, j:j + 1], xprev, ALU.mult, ALU.add).then_inc(mixed, 1)
                dve.wait_ge(mixed, 3)
                dve.wait_ge(act_step, 1)
                step(ts(decay[:, 1:2], decay[:, 0:1], -1.0, None, ALU.mult))
                w = decay[:, 1:2]
                k_, v_, r_ = s(5), s(6), s(7)
                p, p_next = s(0), s(0, 1)
                step(nc.vector.memset(big[:, 0, 0:1], NO_STATE))
                dve.wait_ge(kvr_done, NC)
                step(nc.vector.tensor_tensor_scan(p_next, w.to_broadcast([C, T]), k_, NO_STATE, ALU.add, ALU.max))
                stt(s(1, 1), p, w, p_next, ALU.add, ALU.subtract).then_inc(wkv_arg, 1)
                dve.wait_ge(kvr_ps, NC * 3)
                tt(s(2, 1), k_, p_next, ALU.subtract).then_inc(wkv_arg, 1)
                step(stt(s(3, 1), k_, mix[:, 4:5], p, ALU.add, ALU.max))
                tt(s(4, 1), p, s(3, 1), ALU.subtract).then_inc(wkv_arg, 1)
                dve.wait_ge(wkv_arg, 3)
                stt(s(3, 1), k_, mix[:, 4:5], s(3, 1), ALU.add, ALU.subtract).then_inc(wkv_arg, 1)
                f1, f2, e1, e2 = s(1, 1), s(2, 1), s(4, 1), s(3, 1)
                dve.wait_ge(wkv_arg, 4)
                step(nc.vector.memset(big[:, 0, 0:1], 0.0))
                dve.wait_ge(wkv_exp, 2)
                step(nc.vector.tensor_tensor_scan(s(0, 1), f1, f2, 0.0, ALU.mult, ALU.add))
                dve.wait_ge(kvr_done, NC * 2)
                step(tt(f2, f2, v_, ALU.mult))
                step(nc.vector.memset(big[:, 5, 0:1], 0.0))
                step(nc.vector.tensor_tensor_scan(s(5, 1), f1, f2, 0.0, ALU.mult, ALU.add))
                dve.wait_ge(wkv_exp, 4)
                step(tt(s(0), e1, s(0), ALU.mult))
                step(tt(s(0), s(0), e2, ALU.add))
                step(tt(s(5), e1, s(5), ALU.mult))
                step(tt(e2, e2, v_, ALU.mult))
                step(tt(s(5), s(5), e2, ALU.add))
                step(nc.vector.reciprocal(s(1), s(0)))
                dve.wait_ge(kvr_done, NC * 3)
                step(tt(s(5), s(5), s(1), ALU.mult))
                tt(s(2), s(5), r_, ALU.mult).then_inc(wkv_out, 1)
                for c in range(NC):
                    dve.wait_ge(o_ps, c + 1)
                    tt(x[:, chunk(c)], x[:, chunk(c)], ps[:, 4 + c, :], ALU.add).then_inc(x_ready, 1)

            def quant_ffn(k, before):
                with dve.Fori(0, NC) as c:
                    at = k * NC + c
                    for ht in range(HT1):
                        n = at * HT1 + ht
                        dve.wait_ge(f_sigmoid, n + 1)
                        dve.wait_ge(f_down, PRIME + k * NC + c)
                        tt(f_sig[:, ht, :], f_sig[:, ht, :], ps[:, 2 * ht, :], ALU.mult).then_inc(f_silu, 1)
                        dve.wait_ge(f_silu, n + 1)
                        tt(f_h[:, ht, :], f_sig[:, ht, :], ps[:, 2 * ht + 1, :], ALU.mult).then_inc(f_hid, 1)
                    dve.wait_ge(f_down, PRIME + at + 1)
                    stt(x[:, ds(c * CH, CH)], ps[:, 6, :], 0.5, x[:, ds(c * CH, CH)], ALU.mult, ALU.add).then_inc(x_ready, 1)

            def rms_norm():
                dve.wait_ge(rms_sum, 1)
                ts(ln_v[:, :], ps[:, 4, 0:NT], float(C), None, ALU.mult).then_inc(rms_add, 1)
                dve.wait_ge(rms_std, 1)
                step(ts(ln_s[:, :], ln_s[:, :], RMS_EPS, None, ALU.max))
                step(nc.vector.reciprocal(ln_r[:, :], ln_s[:, :]))
                ts(ln_r[:, :], ln_r[:, :], float(C) ** 0.5, None, ALU.mult).then_inc(rms_rec, 1)
                for c in range(NC):
                    dve.wait_ge(rms_bc, c + 1)
                    stt(xn[:, chunk(c)], xn[:, chunk(c)], gamma1[:, 0:1], ps[:, c, :], ALU.mult, ALU.mult).then_inc(rms_out, 1)

            def split_qk(head, par):
                for c in range(NC):
                    cols = slice(c * CH, c * CH + CH)
                    dve.wait_ge(hi_done, 8 * head + 2 * c + 1)
                    stt(qb[par][0:DH, cols], ps[0:DH, 4 + 2 * (c % 2), :], SCORE_SCALE, qa[par][0:DH, cols].bitcast(fp32),
                        ALU.mult, ALU.subtract).then_inc(lo_done, 1)
                    dve.wait_ge(hi_done, 8 * head + 2 * c + 2)
                    tt(ka[par][DH:128, cols], ps[DH:128, 5 + 2 * (c % 2), :], ka[par][DH:128, cols].bitcast(fp32),
                       ALU.subtract).then_inc(lo_done, 1)
                    nc.vector.tensor_copy(kb[par][0:DH, cols], ka[par][0:DH, cols].bitcast(fp32)).then_inc(kb_done, 1)

            def maxima_chunk(head, c):
                for it in range(NT):
                    dve.wait_ge(s_ps, NC * NT * head + NT * c + it + 1)
                    nc.vector.tensor_reduce(m_part[:, ds(c, 1), it:it + 1].rearrange("p a t -> p (a t)"),
                                            ps[:, 4 + it % 2, :], AX.X, ALU.max).then_inc(s_max, 1)

            def maxima_end(head, par):
                dve.wait_ge(s_max, PRIME + NC * NT * (head + 1))
                nc.vector.tensor_reduce(m_col[par][:, :], m_part[:, :, :].rearrange("p c t -> p t c"),
                                        AX.X, ALU.max, negate=True).then_inc(m_ready, 1)

            def outputs(head, pair, par, c):
                rows = slice(par * DH, par * DH + DH)
                dve.wait_ge(pv_done, GROUPS * (NC * head + c + 1))
                nc.vector.tensor_copy(big[rows, ds(pair, 1), ds(c * CH, CH)].rearrange("p a t -> p (a t)"),
                                      ps[rows, 6, :]).then_inc(o_done, 1)

            def invert(head, par):
                dve.wait_ge(l_loaded, 16 * (head + 1))
                nc.vector.reciprocal(r_col[:, par, :], l_col[:, par, :]).then_inc(r_ready, 1)

            def window(pair, par, with_next, invert_before):
                head = 2 * pair + par
                if with_next:
                    split_qk(head + 1, 1 - par)
                    maxima_chunk(head + 1, 0)
                with dve.Fori(1, NC) as c:
                    outputs(head, pair, par, c - 1)
                    if with_next:
                        maxima_chunk(head + 1, c)
                if with_next:
                    maxima_end(head + 1, 1 - par)
                outputs(head, pair, par, NC - 1)
                if invert_before:
                    invert(head - 1, 1 - par)

            def attention():
                split_qk(0, 0)
                with dve.Fori(0, NC) as c:
                    maxima_chunk(0, c)
                maxima_end(0, 0)
                window(0, 0, True, False)
                window(0, 1, True, True)
                with dve.Fori(1, PAIRS - 1) as pair:
                    window(pair, 0, True, True)
                    window(pair, 1, True, True)
                window(PAIRS - 1, 0, True, True)
                window(PAIRS - 1, 1, False, True)
                invert(HEADS - 1, 1)
                for c in range(NC):
                    dve.wait_ge(out_ps, c + 1)
                    tt(x[:, chunk(c)], x[:, chunk(c)], ps[:, c, :], ALU.add).then_inc(x_ready, 1)

            layer_norm(0)
            moe(0)
            layer_norm(1)
            rwkv()
            layer_norm(2)
            moe(1)
            layer_norm(3)
            dve.wait_ge(l1_loaded, 16 * 4)
            ts(wgu[:, :, :], wgu_i[:, :, :], QUANT_SCALE, None, ALU.mult).then_inc(dequantised, 1)
            ts(wd[:, :, :], wd_i[:, :, :], QUANT_SCALE, None, ALU.mult).then_inc(dequantised, 1)
            step(ts(gamma1[:, :], gamma1[:, :], 1.0, None, ALU.add))
            quant_ffn(0, 3)
            layer_norm(4)
            rms_norm()
            attention()
            layer_norm(5)
            quant_ffn(1, 5)


def kernel(**inputs):
    import numpy as np
    import concourse.bacc as bacc
    from concourse.bass_utils import run_bass_kernel_spmd

    g = {n: np.asarray(v) for n, v in inputs.items()}
    laid = {
        "xT": g["L0_attn_x"][0].T,
        "router_w": g["L0_ffn_router_w"],
        "router_b": g["L0_ffn_router_b"],
        "w1T": g["L0_ffn_w1"].transpose(1, 0, 2),
        "b1T": g["L0_ffn_b1"].reshape(E, HT0, 128).transpose(2, 0, 1),
        "w2T": g["L0_ffn_w2"].reshape(E, HT0, 128, C).transpose(2, 0, 1, 3),
        "b2": g["L0_ffn_b2"],
        "rwkv_wT": np.stack([g["L0_attn_" + n].T for n in ("Wk", "Wv", "Wr", "Wo")], axis=1),
        "mix": np.stack([g["L0_attn_" + n].reshape(C) for n in
                         ("time_mix_k", "time_mix_v", "time_mix_r", "time_decay", "time_first")], axis=1),
        "gamma": g["L1_attn_gamma"].reshape(C, 1),
        "w_qkv": g["L1_attn_w_qkv"],
        "w_outT": g["L1_attn_w_out"].reshape(PAIRS, 128, C).transpose(1, 0, 2),
        "w_gate_upT": np.stack([g["L1_ffn_w_gate"].T, g["L1_ffn_w_up"].T], axis=1),
        "w_downT": g["L1_ffn_w_down"].T.reshape(HT1, 128, C).transpose(1, 0, 2),
    }
    nc = bacc.Bacc("TRN2", target_bir_lowering=False, num_devices=1)
    arrays, aps = {}, {}
    for name, v in laid.items():
        v = np.ascontiguousarray(v)
        arrays[f"in_{name}"] = v
        aps[name] = nc.dram_tensor(f"in_{name}", v.shape, mybir.dt.from_np(v.dtype), kind="ExternalInput").ap()
    out = nc.dram_tensor("out_xT", (C, T), fp32, kind="ExternalOutput").ap()
    l_scratch = nc.dram_tensor("l_scratch", (HEADS, T), fp32, kind="Internal").ap()
    r_scratch = nc.dram_tensor("r_scratch", (HEADS, T), fp32, kind="Internal").ap()
    macaron_kernel(nc, aps, out, l_scratch, r_scratch)
    r = run_bass_kernel_spmd(nc, [arrays], core_ids=[0])
    return np.ascontiguousarray(r.results[0]["out_xT"].T).reshape(1, T, C)
```

```python
import concourse.bass as bass
from concourse import mybir
from concourse.alu_op_type import AluOpType as ALU
from contextlib import ExitStack

fp32 = mybir.dt.float32
fp32r = mybir.dt.float32r
int32 = mybir.dt.int32
ACT = mybir.ActivationFunctionType
AX = mybir.AxisListType
ds = bass.ds

C = 128
T = 2048
CH = 512
NC = T // CH
NT = T // 128
TPC = CH // 128
E, H0 = 8, 512
HT0 = H0 // 128
UNITS = E * HT0
HEADS, DH = 16, 64
PAIRS = HEADS // 2
H1 = 384
HT1 = H1 // 128
GROUPS = NT // 2
LN_EPS = 1e-5
RMS_EPS = 1e-12
QUANT_SCALE = 1.0 / 127.0
SCORE_SCALE = DH ** -0.5
NO_STATE = -1e38
EXCLUDE = -3.0e38
LAG = 4
PV_LAG = 2
PRIME = 1
WKV_SLOTS = (1, 2, 4, 3)




def macaron_kernel(nc, a, out, g_scratch, l_scratch, r_scratch):
    ctx = ExitStack()
    with ctx:
        def sb(name, shape, dt=fp32, where=ctx):
            return where.enter_context(nc.sbuf_tensor(name, shape, dt))

        def sem(name):
            return ctx.enter_context(nc.semaphore(name))

        x = sb("x", [C, T])
        xnp = sb("xnp", [C, T + 1])
        xn = xnp[:, 1:T + 1]
        xprev = xnp[:, 0:T]
        x_h = sb("x_h", [C, T], fp32r)
        x_l = sb("x_l", [C, T], fp32r)
        cen = sb("cen", [C, T])
        sqr = sb("sqr", [C, T])
        ident = sb("ident", [128, 128])
        inv_c = sb("inv_c", [128, 128])
        ln_v = sb("ln_v", [128, NT])
        ln_s = sb("ln_s", [128, NT])
        ln_r = sb("ln_r", [128, NT])
        gamma1 = sb("gamma1", [C, 1])

        one = ExitStack()
        big = sb("big", [C, 8, T + 8], where=one)
        w1_h = sb("w1_h", [C, E, H0], fp32r, one)
        w1_l = sb("w1_l", [C, E, H0], fp32r, one)
        w2_h = sb("w2_h", [128, E, HT0, C], fp32r, one)
        w2_l = sb("w2_l", [128, E, HT0, C], fp32r, one)
        b1 = sb("b1", [128, E, HT0], where=one)
        b2 = sb("b2", [C, E], where=one)
        rw = sb("rw", [C, E], where=one)
        rb = sb("rb", [128, E], where=one)
        rank = sb("rank", [128, E], where=one)
        lg = sb("lg", [128, NT, E], where=one)
        lg2 = sb("lg2", [128, NT, E], where=one)
        eq = sb("eq", [128, NT, E], where=one)
        best = sb("best", [128, NT, E], where=one)
        second = sb("second", [128, NT, E], where=one)
        gates = sb("gates", [128, NT, E], where=one)
        rt = sb("rt", [128, 8, NT], where=one)
        h_h = sb("h_h", [128, 4, CH], fp32r, one)
        h_l = sb("h_l", [128, 4, CH], fp32r, one)
        rwkv_w = sb("rwkv_w", [C, 4, C], where=one)
        mix = sb("mix", [C, 5], where=one)
        decay = sb("decay", [C, 2], where=one)
        one.close()
        flat = big[:, :, :].rearrange("p a n -> p (a n)")
        S1 = T + 8
        g_bc = flat[:, 0:E * CH].rearrange("p (e n) -> p e n", e=E)
        w1_raw = flat[:, 2 * S1:2 * S1 + E * H0].rearrange("p (e n) -> p e n", e=E)
        w2_raw = flat[:, 4 * S1:4 * S1 + E * H0].rearrange("p (e a n) -> p e a n", e=E, a=HT0)
        h_raw = big[:, 6, 0:4 * CH].rearrange("p (a n) -> p a n", a=4)
        g_t = big[0:E, 7, 0:T]
        y_gated = sqr[:, 0:2 * CH].rearrange("p (a n) -> p a n", a=2)

        two = ExitStack()
        wgu_i = sb("wgu_i", [C, 2, H1], int32, two)
        wd_i = sb("wd_i", [128, HT1, C], int32, two)
        wgu = sb("wgu", [C, 2, H1], fp32r, two)
        wd = sb("wd", [128, HT1, C], fp32r, two)
        ka = [sb(f"ka{i}", [128, T], fp32r, two) for i in range(2)]
        kb = [sb(f"kb{i}", [DH + 1, T], fp32r, two) for i in range(2)]
        qa = [sb(f"qa{i}", [128, T], fp32r, two) for i in range(2)]
        qb = [sb(f"qb{i}", [DH + 1, T], fp32r, two) for i in range(2)]
        v_h = sb("v_h", [128, 2, NT, DH + 1], fp32r, two)
        v_l = sb("v_l", [128, 2, NT, DH + 1], fp32r, two)
        p_raw = sb("p_raw", [128, 2, 2, CH], where=two)
        p_h = sb("p_h", [128, 4, 2, CH], fp32r, two)
        p_l = sb("p_l", [128, 4, 2, CH], fp32r, two)
        qk_raw = [sb(f"qk_raw{i}", [C, 2, DH], where=two) for i in range(2)]
        qk_h = [sb(f"qk_h{i}", [C, 2, 2, DH], fp32r, two) for i in range(2)]
        qk_l = [sb(f"qk_l{i}", [C, 2, 2, DH], fp32r, two) for i in range(2)]
        wv_raw = sb("wv_raw", [C, 2 * DH], where=two)
        wv_h = sb("wv_h", [C, 2 * DH], fp32r, two)
        wv_l = sb("wv_l", [C, 2 * DH], fp32r, two)
        w_o = sb("w_o", [128, C], where=two)
        m_part = sb("m_part", [128, NC, NT], where=two)
        m_col = [sb(f"m_col{i}", [128, NT], where=two) for i in range(2)]
        m_t = sb("m_t", [NT, 128], fp32r, two)
        l_row = sb("l_row", [DH + 1, T], where=two)
        l_col = sb("l_col", [128, 2, NT], where=two)
        r_col = sb("r_col", [128, 2, NT], where=two)
        two.close()
        o_raw, o_nrm, r_bc = cen, sqr, xn
        f_sig = p_raw[:, :, :, :].rearrange("p a b n -> p (a b) n")
        f_hid = cen[:, 0:HT1 * CH].rearrange("p (a n) -> p a n", a=HT1)
        f_h = p_h[:, 0:2, :, :].rearrange("p a b n -> p (a b) n")
        f_l = p_l[:, 0:2, :, :].rearrange("p a b n -> p (a b) n")

        ps = ctx.enter_context(nc.psum_tensor("ps", [128, 8, CH], fp32))

        x_loaded = sem("x_loaded")
        small_loaded = sem("small_loaded")
        w1_loaded, w2_loaded = sem("w1_loaded"), sem("w2_loaded")
        l1_loaded = sem("l1_loaded")
        const_step, const_ready = sem("const_step"), sem("const_ready")
        l1_const, dequantised = sem("l1_const"), sem("dequantised")
        x_ready = sem("x_ready")
        dve_step = sem("dve_step")
        act_step = sem("act_step")
        ln_mean, ln_cen, ln_sq, ln_var = sem("ln_mean"), sem("ln_cen"), sem("ln_sq"), sem("ln_var")
        ln_add, ln_std, ln_rec, ln_bc, ln_out = sem("ln_add"), sem("ln_std"), sem("ln_rec"), sem("ln_bc"), sem("ln_out")
        xh_done, xl_done = sem("xh_done"), sem("xl_done")
        w_hi, w_lo = sem("w_hi"), sem("w_lo")
        rt_logits, rt_diff, rt_exp, rt_gates = sem("rt_logits"), sem("rt_diff"), sem("rt_exp"), sem("rt_gates")
        gt_ps, gt_done, g_stored = sem("gt_ps"), sem("gt_done"), sem("g_stored")
        g_loaded = [sem(f"g_loaded{e}") for e in range(E)]
        h_ps, h_relu, h_hi, h_hi2, h_done = sem("h_ps"), sem("h_relu"), sem("h_hi"), sem("h_hi2"), sem("h_done")
        w2_done, y_gate, y_add = sem("w2_done"), sem("y_gate"), sem("y_add")
        mixed, kvr_ps, kvr_done, wkv_arg, wkv_exp = sem("mixed"), sem("kvr_ps"), sem("kvr_done"), sem("wkv_arg"), sem("wkv_exp")
        wkv_out, o_ps = sem("wkv_out"), sem("o_ps")
        f_ps, f_sigmoid, f_silu, f_prod, f_hi, f_lo, f_down = (
            sem("f_ps"), sem("f_sigmoid"), sem("f_silu"), sem("f_prod"), sem("f_hi"), sem("f_lo"), sem("f_down"))
        rms_sq, rms_sum, rms_add, rms_std, rms_rec, rms_bc, rms_out = (
            sem("rms_sq"), sem("rms_sum"), sem("rms_add"), sem("rms_std"), sem("rms_rec"), sem("rms_bc"), sem("rms_out"))
        qk_loaded = [sem("qk_loaded0"), sem("qk_loaded1")]
        wv_loaded, wo_loaded = sem("wv_loaded"), sem("wo_loaded")
        qkw_hi, qkw_lo, vw_hi, vw_lo = sem("qkw_hi"), sem("qkw_lo"), sem("vw_hi"), sem("vw_lo")
        v_ps, v_hi, v_lo = sem("v_ps"), sem("v_hi"), sem("v_lo")
        proj_ps, hi_done, lo_done, kb_done = sem("proj_ps"), sem("hi_done"), sem("lo_done"), sem("kb_done")
        m_ready, mt_ps, mt_done, m_loaded = sem("m_ready"), sem("mt_ps"), sem("mt_done"), sem("m_loaded")
        st_ps, exp_done, ph_done, pl_even, pl_odd, pv_done = (
            sem("st_ps"), sem("exp_done"), sem("ph_done"), sem("pl_even"), sem("pl_odd"), sem("pv_done"))
        s_ps, s_max = sem("s_ps"), sem("s_max")
        o_done, l_done = sem("o_done"), sem("l_done")
        l_stored, l_loaded, r_ready, r_stored, r_loaded, o_scaled = (
            sem("l_stored"), sem("l_loaded"), sem("r_ready"), sem("r_stored"), sem("r_loaded"), sem("o_scaled"))
        out_ps, out_add = sem("out_ps"), sem("out_add")
        stored = sem("stored")

        block = ctx.enter_context(nc.Block())

        def chunk(c):
            return ds(c * CH, CH)

        def wait_x(eng, k):
            if k == 0:
                eng.wait_ge(x_loaded, 16)
            else:
                eng.wait_ge(x_ready, PRIME + NC * k)

        @block.sync
        def _(sp):
            sp.dma_start(x[:, :], a["xT"]).then_inc(x_loaded, 16)
            sp.dma_start(rw[:, :], a["router_w"]).then_inc(small_loaded, 16)
            sp.dma_start(rb[:, :], a["router_b"].rearrange("(a e) -> a e", a=1).to_broadcast([128, E])).then_inc(small_loaded, 16)
            sp.dma_start(b1[:, :, :], a["b1T"]).then_inc(small_loaded, 16)
            sp.dma_start(b2[:, :], a["b2T"]).then_inc(small_loaded, 16)
            sp.dma_start(rwkv_w[:, :, :], a["rwkv_wT"]).then_inc(small_loaded, 16)
            sp.dma_start(mix[:, :], a["mix"]).then_inc(small_loaded, 16)
            sp.dma_start(w1_raw, a["w1T"]).then_inc(w1_loaded, 16)
            sp.dma_start(w2_raw, a["w2T"]).then_inc(w2_loaded, 16)
            sp.dma_start(gamma1[:, :], a["gamma"]).then_inc(l1_loaded, 16)

            def gates_everywhere(k):
                sp.wait_ge(gt_done, NC * (k + 1))
                sp.dma_start(g_scratch[k, :, :], g_t).then_inc(g_stored, 16)
                sp.wait_ge(g_stored, 16 * (k + 1))
                for e in range(E):
                    if k > 0:
                        sp.wait_ge(y_gate, PRIME + E * NC * k)
                    sp.dma_start(g_bc[:, e, :], g_scratch[k, e:e + 1, 0:CH].to_broadcast([128, CH])).then_inc(g_loaded[e], 16)
                with sp.Fori(1, NC) as c:
                    for e in range(E):
                        sp.wait_ge(y_gate, PRIME + E * (NC * k + c - 1) + e + 1)
                        sp.dma_start(g_bc[:, e, :], g_scratch[k, e:e + 1, ds(c * CH, CH)].to_broadcast([128, CH])).then_inc(g_loaded[e], 16)

            gates_everywhere(0)
            gates_everywhere(1)
            sp.wait_ge(x_ready, PRIME + NC * 3)
            sp.dma_start(wgu_i[:, :, :], a["w_gate_upT"]).then_inc(l1_loaded, 16)
            sp.dma_start(wd_i[:, :, :], a["w_downT"]).then_inc(l1_loaded, 16)

            def maxima_row(head, par):
                sp.wait_ge(mt_done, head + 1)
                sp.dma_start(qb[par][DH:DH + 1, :].bitcast(fp32), m_t[:, :].bitcast(fp32)).then_inc(m_loaded, 16)

            def normalise(head, par):
                sp.wait_ge(l_done, PRIME + NC * (head + 1))
                sp.dma_start(l_scratch[ds(head, 1), :], l_row[DH:DH + 1, :]).then_inc(l_stored, 16)
                sp.wait_ge(l_stored, 16 * (head + 1))
                sp.dma_start(l_col[:, par, :], l_scratch[ds(head, 1), :].rearrange("a (p t) -> (a p) t", p=128)).then_inc(l_loaded, 16)
                sp.wait_ge(r_ready, head + 1)
                sp.dma_start(r_scratch[ds(head, 1), :].rearrange("a (p t) -> (a p) t", p=128), r_col[:, par, :]).then_inc(r_stored, 16)
                sp.wait_ge(r_stored, 16 * (head + 1))
                sp.wait_ge(o_scaled, PRIME + NC * head)
                sp.dma_start(r_bc[par * DH:par * DH + DH, :],
                             r_scratch[ds(head, 1), :].to_broadcast([DH, T])).then_inc(r_loaded, 16)

            maxima_row(0, 0)
            maxima_row(1, 1)
            with sp.Fori(0, PAIRS - 1) as pair:
                normalise(2 * pair, 0)
                maxima_row(2 * pair + 2, 0)
                normalise(2 * pair + 1, 1)
                maxima_row(2 * pair + 3, 1)
            normalise(HEADS - 2, 0)
            normalise(HEADS - 1, 1)
            for c in range(NC):
                sp.wait_ge(x_ready, PRIME + NC * 5 + c + 1)
                sp.dma_start(out[:, chunk(c)], x[:, chunk(c)]).then_inc(stored, 16)
            sp.wait_ge(stored, 16 * NC)

        @block.gpsimd
        def _(pool):
            nc.gpsimd.memset(ident[:, :], 0.0).then_inc(const_step, 1)
            nc.gpsimd.memset(inv_c[:, :], 1.0 / C).then_inc(const_ready, 1)
            nc.gpsimd.memset(xnp[:, 0:1], 0.0).then_inc(const_ready, 1)
            for e in range(E):
                nc.gpsimd.memset(rank[:, e:e + 1], float(E - e)).then_inc(const_ready, 1)
            pool.wait_ge(const_step, 1)
            nc.gpsimd.affine_select(out=ident[:, :], in_=ident[:, :], compare_op=ALU.not_equal, fill=1.0,
                                    base=0, pattern=[[-1, 128]], channel_multiplier=1).then_inc(const_ready, 1)
            pool.wait_ge(x_ready, PRIME + NC * 3)
            for i in range(2):
                nc.gpsimd.memset(kb[i][DH:DH + 1, :].bitcast(fp32), 1.0).then_inc(l1_const, 1)
            pool.wait_ge(l1_const, 2)
            nc.gpsimd.memset(v_h[:, :, :, DH:DH + 1].bitcast(fp32), 1.0).then_inc(l1_const, 1)
            nc.gpsimd.memset(v_l[:, :, :, DH:DH + 1].bitcast(fp32), 0.0).then_inc(l1_const, 1)

            def quant_ffn(k):
                with pool.Fori(0, NC) as c:
                    at = k * NC + c
                    for ht in range(HT1):
                        pool.wait_ge(f_hi, at * HT1 + ht + 1)
                        pool.wait_ge(f_down, PRIME + at)
                        nc.gpsimd.tensor_tensor(f_l[:, ht, :], f_hid[:, ht, :], f_h[:, ht, :].bitcast(fp32),
                                                ALU.subtract).then_inc(f_lo, 1)

            def low_part(head, c, g, first):
                n = GROUPS * (NC * head + c) + g
                pool.wait_ge(ph_done, n + 1)
                if not first or g >= 4:
                    pool.wait_ge(pv_done, n - 3)
                nc.gpsimd.tensor_tensor(p_l[:, g % 4, 1, :], p_raw[:, g % 2, 1, :], p_h[:, g % 4, 1, :].bitcast(fp32),
                                        ALU.subtract).then_inc(pl_odd, 1)

            def scale(head, par, piece, low_parts, wait_out=None):
                rows = slice(par * DH, par * DH + DH)
                pool.wait_ge(r_loaded, 16 * (head + 1))
                pool.wait_ge(o_done, PRIME + NC * (head + 1))
                if wait_out is not None:
                    pool.wait_ge(out_ps, PRIME + wait_out)
                pool.wait_ge(pl_odd, low_parts)
                nc.gpsimd.tensor_tensor(o_nrm[rows, ds(piece * CH, CH)], o_raw[rows, ds(piece * CH, CH)],
                                        r_bc[rows, ds(piece * CH, CH)], ALU.mult).then_inc(o_scaled, 1)
                pool.wait_ge(o_scaled, PRIME + NC * head + piece + 1)

            def window(pair, par, scale_before):
                head = 2 * pair + par
                for g in range(GROUPS):
                    low_part(head, 0, g, True)

                later = not (isinstance(pair, int) and pair == 0)

                def piece(q, low_parts):
                    scale(head - 1, 1 - par, q, low_parts, NC * (pair - 1) + q + 1 if par == 1 and later else None)
                with pool.Fori(1, NC) as c:
                    for g in range(GROUPS):
                        low_part(head, c, g, False)
                        if g == 1 and scale_before:
                            piece(c - 1, GROUPS * (NC * head + c) + g + 1)
                if scale_before:
                    piece(NC - 1, GROUPS * NC * (head + 1))

            def attention():
                window(0, 0, False)
                window(0, 1, True)
                with pool.Fori(1, PAIRS) as pair:
                    window(pair, 0, True)
                    window(pair, 1, True)
                for q in range(NC):
                    scale(HEADS - 1, 1, q, GROUPS * NC * HEADS)

            quant_ffn(0)
            attention()
            quant_ffn(1)
        CONST = 2 + E + 1
        L1_CONST = 4

        @block.tensor
        def _(pe):
            mm = nc.tensor.matmul

            def layer_norm(k):
                wait_x(pe, k)
                if k == 0:
                    pe.wait_ge(const_ready, CONST)
                for c in range(NC):
                    mm(ps[:, c, :], inv_c[:, :], x[:, chunk(c)], start=True, stop=True).then_inc(ln_mean, 1)
                for c in range(NC):
                    pe.wait_ge(ln_sq, NC * k + c + 1)
                    for t in range(TPC * c, TPC * c + TPC):
                        last = mm(ps[:, 4, t:t + 1], sqr[:, t * 128:t * 128 + 128], inv_c[:, 0:1], start=True, stop=True)
                last.then_inc(ln_var, 1)
                pe.wait_ge(ln_rec, k + 1)
                for c in range(NC):
                    for t in range(TPC):
                        last = mm(ps[:, c, t * 128:t * 128 + 128],
                                  ln_r[:, TPC * c + t:TPC * c + t + 1].to_broadcast([128, 128]), ident[:, :], start=True, stop=True)
                    last.then_inc(ln_bc, 1)

            def split_product(o, w_hi_, w_lo_, x_hi_, x_lo_, start, stop):
                mm(o, w_lo_, x_hi_, start=start, stop=False)
                mm(o, w_hi_, x_hi_, start=False, stop=False)
                return mm(o, w_hi_, x_lo_, start=False, stop=stop)

            def moe(k):
                pe.wait_ge(ln_out, NC * (k * 2 + 1))
                pe.wait_ge(small_loaded, 16 * 6)
                for t in range(NT):
                    last = mm(ps[:, 5, t * E:t * E + E], xn[:, t * 128:t * 128 + 128], rw[:, :], start=True, stop=True)
                last.then_inc(rt_logits, 1)
                pe.wait_ge(rt_gates, k + 1)
                for c in range(NC):
                    for t in range(TPC):
                        last = mm(ps[0:E, c, t * 128:t * 128 + 128], gates[:, TPC * c + t, :], ident[:, :], start=True, stop=True)
                    last.then_inc(gt_ps, 1)
                pe.wait_ge(gt_done, NC * (k + 1))
                pe.wait_ge(xl_done, NC * (k + 1))
                if k == 0:
                    pe.wait_ge(w_lo, 2)
                with pe.Fori(0, NC) as c:
                    at = (k * NC + c)

                    def second_product(u):
                        e, ht = u // HT0, u % HT0
                        if ht == 0:
                            pe.wait_ge(y_gate, PRIME + at * E + max(e - 1, 0))
                        pe.wait_ge(h_done, PRIME + at * UNITS + u + 1)
                        split_product(ps[:, 4 + e % 2, :], w2_h[:, e, ht, :], w2_l[:, e, ht, :], h_h[:, u % 4, :], h_l[:, u % 4, :],
                                      ht == 0, ht == HT0 - 1).then_inc(w2_done, 1)
                    for u in range(UNITS):
                        e, ht = u // HT0, u % HT0
                        pe.wait_ge(h_relu, PRIME + at * UNITS + max(u - 3, 0))
                        cols = slice(ht * 128, ht * 128 + 128)
                        split_product(ps[:, u % 4, :], w1_h[:, e, cols], w1_l[:, e, cols], x_h[:, chunk(c)], x_l[:, chunk(c)],
                                      True, True).then_inc(h_ps, 1)
                        if u >= LAG:
                            second_product(u - LAG)
                    for u in range(UNITS - LAG, UNITS):
                        second_product(u)

            def rwkv():
                for j in range(3):
                    pe.wait_ge(mixed, j + 1)
                    for c in range(NC):
                        if j == 2:
                            pe.wait_ge(kvr_done, c + 1)
                        mm(ps[:, (4 if j == 1 else 0) + c, :], rwkv_w[:, j, :], big[:, 2 + j, ds(c * CH, CH)],
                           start=True, stop=True).then_inc(kvr_ps, 1)
                pe.wait_ge(wkv_out, 1)
                for c in range(NC):
                    mm(ps[:, 4 + c, :], rwkv_w[:, 3, :], big[:, 2, ds(c * CH, CH)], start=True, stop=True).then_inc(o_ps, 1)

            def quant_ffn(k, before):
                pe.wait_ge(xl_done, NC * (2 * k + 3))
                pe.wait_ge(dequantised, 2)
                with pe.Fori(0, NC) as c:
                    at = k * NC + c
                    for ht in range(HT1):
                        if ht == 0:
                            pe.wait_ge(f_prod, PRIME + at * HT1)
                        for g in range(2):
                            w = wgu[:, g, ht * 128:ht * 128 + 128]
                            mm(ps[:, 2 * ht + g, :], w, x_h[:, chunk(c)], start=True, stop=False)
                            last = mm(ps[:, 2 * ht + g, :], w, x_l[:, chunk(c)], start=False, stop=True)
                        last.then_inc(f_ps, 1)
                    pe.wait_ge(x_ready, PRIME + NC * before + c)
                    for ht in range(HT1):
                        pe.wait_ge(f_lo, at * HT1 + ht + 1)
                        mm(ps[:, 6, :], wd[:, ht, :], f_h[:, ht, :], start=(ht == 0), stop=False)
                        last = mm(ps[:, 6, :], wd[:, ht, :], f_l[:, ht, :], start=False, stop=(ht == HT1 - 1))
                    last.then_inc(f_down, 1)

            def rms_norm():
                for c in range(NC):
                    pe.wait_ge(rms_sq, c + 1)
                    for t in range(TPC * c, TPC * c + TPC):
                        last = mm(ps[:, 4, t:t + 1], sqr[:, t * 128:t * 128 + 128], inv_c[:, 0:1], start=True, stop=True)
                last.then_inc(rms_sum, 1)
                pe.wait_ge(rms_rec, 1)
                for c in range(NC):
                    for t in range(TPC):
                        last = mm(ps[:, c, t * 128:t * 128 + 128],
                                  ln_r[:, TPC * c + t:TPC * c + t + 1].to_broadcast([128, 128]), ident[:, :], start=True, stop=True)
                    last.then_inc(rms_bc, 1)

            QK_BANKS = (4, 5, 0, 1)

            def project_qk(head, par, i, start_of_window=False):
                c, s = i // 2, i % 2
                w_hi_ = qk_h[par][:, s, :, :].rearrange("p a d -> p (a d)")
                w_lo_ = qk_l[par][:, s, :, :].rearrange("p a d -> p (a d)")
                cols = slice(c * CH, c * CH + CH)
                if i >= 4 or start_of_window:
                    pe.wait_ge(lo_done, 8 * head + i - 3)
                split_product(ps[:, QK_BANKS[i % 4], :], w_hi_, w_lo_, x_h[:, cols], x_l[:, cols], True, True).then_inc(proj_ps, 1)

            def project_v(pair):
                pe.wait_ge(vw_lo, pair + 1)
                for t in range(NT):
                    bank, col = 2 + (t // 4) % 2, (t % 4) * 128
                    tile = slice(t * 128, t * 128 + 128)
                    if t % 4 == 0 and t >= 8:
                        pe.wait_ge(v_lo, 4 * pair + t // 4 - 1)
                    o = ps[:, bank, col:col + 128]
                    mm(o, x_h[:, tile], wv_l[:, :], start=True, stop=False)
                    mm(o, x_h[:, tile], wv_h[:, :], start=False, stop=False)
                    last = mm(o, x_l[:, tile], wv_h[:, :], start=False, stop=True)
                    if t % 4 == 3:
                        last.then_inc(v_ps, 1)

            def score_tile(head, par, c, it):
                if it < 2:
                    pe.wait_ge(s_max, PRIME + NC * NT * head + NT * c)
                else:
                    pe.wait_ge(s_max, PRIME + NC * NT * head + NT * c + it - 1)
                mm(ps[:, 4 + it % 2, :], qa[par][:, it * 128:it * 128 + 128], ka[par][:, ds(c * CH, CH)],
                   start=True, stop=True).then_inc(s_ps, 1)

            def turn_maxima(head, par):
                pe.wait_ge(m_ready, head + 1)
                mm(ps[0:NT, 7, 0:128], m_col[par][:, :], ident[:, :], start=True, stop=True).then_inc(mt_ps, 1)

            def values(head, par, c, g):
                n = GROUPS * (NC * head + c) + g
                pe.wait_ge(pl_even, n + 1)
                pe.wait_ge(pl_odd, n + 1)
                if g == 0:
                    pe.wait_ge(o_done, PRIME + NC * head + c)
                    pe.wait_ge(l_done, PRIME + NC * head + c)
                for j in range(2):
                    jt = 2 * g + j
                    last = split_product(ps[0:DH + 1, 6, :], v_h[:, par, jt, :], v_l[:, par, jt, :],
                                         p_h[:, g % 4, j, :], p_l[:, g % 4, j, :], jt == 0, jt == NT - 1)
                last.then_inc(pv_done, 1)

            def scores_t(head, par, c, g):
                for j in range(2):
                    jt = 2 * g + j
                    st = ps[:, 2 * (g % 2) + j, :]
                    mm(st, ka[par][:, jt * 128:jt * 128 + 128], qa[par][:, ds(c * CH, CH)], start=True, stop=False)
                    last = mm(st, kb[par][:, jt * 128:jt * 128 + 128], qb[par][:, ds(c * CH, CH)], start=False, stop=True)
                last.then_inc(st_ps, 1)

            def project_out(pair, c, bank):
                mm(ps[:, bank, :], w_o[:, :], o_nrm[:, ds(c * CH, CH)], start=True, stop=True).then_inc(out_ps, 1)

            def main_chunk(pair, par, c, first, with_next, with_out):
                head = 2 * pair + par
                n0 = GROUPS * (NC * head + c)
                for g in range(GROUPS):
                    if not first or g >= 2:
                        pe.wait_ge(exp_done, n0 + g - 1)
                    if first and g == 1:
                        pe.wait_ge(v_lo, 4 * (pair + 1))
                    scores_t(head, par, c, g)
                    if g < PV_LAG and not first:
                        values(head, par, c - 1, GROUPS - PV_LAG + g)
                    if with_next:
                        for it in (2 * g, 2 * g + 1):
                            score_tile(head + 1, 1 - par, c, it)
                    if g >= PV_LAG:
                        values(head, par, c, g - PV_LAG)
                    if g == 5 and with_out:
                        if first:
                            pe.wait_ge(o_scaled, PRIME + NC * head - NC)
                            pe.wait_ge(wo_loaded, 16 * pair)
                        pe.wait_ge(out_add, PRIME + NC * (pair - 1) + c)
                        project_out(pair - 1, c, 7)

            def window(pair, par, with_next, project, with_v):
                head = 2 * pair + par
                with_out = par == 1 and not (isinstance(pair, int) and pair == 0)
                pe.wait_ge(m_loaded, 16 * (head + 1))
                pe.wait_ge(kb_done, NC * (head + 1))
                pe.wait_ge(lo_done, 8 * (head + 2) if with_next else 8 * (head + 1))
                if with_next:
                    pe.wait_ge(kb_done, NC * (head + 2))
                main_chunk(pair, par, 0, True, with_next, with_out)
                with pe.Fori(1, NC) as c:
                    main_chunk(pair, par, c, False, with_next, with_out)
                n0 = GROUPS * NC * head + GROUPS * (NC - 1)
                if project:
                    pe.wait_ge(qkw_lo, head + 3)
                    pe.wait_ge(s_max, PRIME + NC * NT * (head + 2))
                    project_qk(head + 2, par, 0)
                    project_qk(head + 2, par, 1)
                    pe.wait_ge(exp_done, n0 + GROUPS - 1)
                    project_qk(head + 2, par, 2)
                    project_qk(head + 2, par, 3)
                if with_next:
                    turn_maxima(head + 1, 1 - par)
                values(head, par, NC - 1, GROUPS - 2)
                if project:
                    project_qk(head + 2, par, 4)
                    project_qk(head + 2, par, 5)
                values(head, par, NC - 1, GROUPS - 1)
                if project:
                    project_qk(head + 2, par, 6)
                    project_qk(head + 2, par, 7)
                if with_v:
                    project_v(pair + 1)

            def attention():
                pe.wait_ge(xl_done, NC * 4)
                pe.wait_ge(l1_const, L1_CONST)
                for head in range(2):
                    pe.wait_ge(qkw_lo, head + 1)
                    for i in range(8):
                        project_qk(head, head, i, head == 1)
                project_v(0)
                pe.wait_ge(lo_done, 16)
                with pe.Fori(0, NC) as c:
                    for it in range(NT):
                        score_tile(0, 0, c, it)
                turn_maxima(0, 0)
                window(0, 0, True, True, False)
                window(0, 1, True, True, True)
                with pe.Fori(1, PAIRS - 1) as pair:
                    window(pair, 0, True, True, False)
                    window(pair, 1, True, True, True)
                window(PAIRS - 1, 0, True, False, False)
                window(PAIRS - 1, 1, False, False, False)
                pe.wait_ge(wo_loaded, 16 * PAIRS)
                for c in range(NC):
                    pe.wait_ge(o_scaled, PRIME + NC * (HEADS - 1) + c + 1)
                    project_out(PAIRS - 1, c, c)

            layer_norm(0)
            moe(0)
            layer_norm(1)
            rwkv()
            layer_norm(2)
            moe(1)
            layer_norm(3)
            quant_ffn(0, 3)
            layer_norm(4)
            rms_norm()
            attention()
            layer_norm(5)
            quant_ffn(1, 5)

        @block.scalar
        def _(act):
            af = nc.scalar.activation

            def layer_norm(k):
                for c in range(NC):
                    act.wait_ge(ln_cen, NC * k + c + 1)
                    af(sqr[:, chunk(c)], cen[:, chunk(c)], ACT.Square).then_inc(ln_sq, 1)
                act.wait_ge(ln_add, k + 1)
                af(ln_s[:, :], ln_v[:, :], ACT.Sqrt).then_inc(ln_std, 1)

            def high_parts(j):
                for c in range(NC):
                    if j == 3:
                        act.wait_ge(rms_out, c + 1)
                    else:
                        act.wait_ge(ln_out, NC * (0, 2, 3, 0, 5)[j] + c + 1)
                    af(x_h[:, chunk(c)], xn[:, chunk(c)], ACT.Copy).then_inc(xh_done, 1)

            def split_weights():
                act.wait_ge(w1_loaded, 16)
                af(w1_h[:, :, :], w1_raw, ACT.Copy).then_inc(w_hi, 1)
                act.wait_ge(w2_loaded, 16)
                af(w2_h[:, :, :, :].rearrange("p e a n -> p (e a n)"), w2_raw.rearrange("p e a n -> p (e a n)"),
                   ACT.Copy).then_inc(w_hi, 1)

            def moe(k):
                high_parts(k)
                if k == 0:
                    split_weights()
                act.wait_ge(rt_diff, k + 1)
                af(rt[:, 3, :], rt[:, 2, :], ACT.Exp).then_inc(rt_exp, 1)
                for c in range(NC):
                    act.wait_ge(gt_ps, NC * k + c + 1)
                    af(g_t[:, chunk(c)], ps[0:E, c, :], ACT.Copy).then_inc(gt_done, 1)
                with act.Fori(0, NC) as c:
                    at = k * NC + c
                    for u in range(UNITS):
                        e, ht = u // HT0, u % HT0
                        act.wait_ge(h_ps, at * UNITS + u + 1)
                        act.wait_ge(h_done, PRIME + at * UNITS + max(u - 3, 0))
                        af(h_raw[:, u % 4, :], ps[:, u % 4, :], ACT.Relu, bias=b1[:, e, ht:ht + 1]).then_inc(h_relu, 1)
                        if u % 2 == 1:
                            act.wait_ge(h_relu, PRIME + at * UNITS + u)
                            act.wait_ge(w2_done, PRIME + at * UNITS + max(u - 4, 0))
                            af(h_h[:, (u - 1) % 4, :], h_raw[:, (u - 1) % 4, :], ACT.Copy).then_inc(h_hi, 1)

            def rwkv():
                act.wait_ge(small_loaded, 16 * 6)
                af(decay[:, 0:1], mix[:, 3:4], ACT.Exp).then_inc(act_step, 1)
                for j in range(3):
                    for c in range(NC):
                        act.wait_ge(kvr_ps, NC * j + c + 1)
                        src = ps[:, (4 if j == 1 else 0) + c, :]
                        af(big[:, 5 + j, ds(c * CH, CH)], src, ACT.Copy if j < 2 else ACT.Sigmoid).then_inc(kvr_done, 1)
                for n in range(4):
                    act.wait_ge(wkv_arg, n + 1)
                    s = WKV_SLOTS[n]
                    af(big[:, s, 1:T + 1], big[:, s, 1:T + 1], ACT.Exp).then_inc(wkv_exp, 1)

            def quant_ffn(k):
                high_parts(2 * k + 2)
                with act.Fori(0, NC) as c:
                    at = k * NC + c
                    for ht in range(HT1):
                        act.wait_ge(f_ps, at * HT1 + ht + 1)
                        af(f_sig[:, ht, :], ps[:, 2 * ht, :], ACT.Sigmoid, scale=QUANT_SCALE).then_inc(f_sigmoid, 1)
                    for ht in range(HT1):
                        act.wait_ge(f_prod, PRIME + at * HT1 + ht + 1)
                        act.wait_ge(f_down, PRIME + at)
                        af(f_h[:, ht, :], f_hid[:, ht, :], ACT.Copy).then_inc(f_hi, 1)

            def rms_norm():
                for c in range(NC):
                    act.wait_ge(ln_out, NC * 4 + c + 1)
                    af(sqr[:, chunk(c)], xn[:, chunk(c)], ACT.Square).then_inc(rms_sq, 1)
                act.wait_ge(rms_add, 1)
                af(ln_s[:, :], ln_v[:, :], ACT.Sqrt).then_inc(rms_std, 1)

            def load_qk(head, par):
                for s in range(2):
                    act.dma_start(qk_raw[par][:, s, :],
                                  a["w_qkv"][:, ds(head * DH + s * HEADS * DH, DH)]).then_inc(qk_loaded[par], 16)

            def load_v(pair):
                act.dma_start(wv_raw[:, :], a["w_qkv"][:, ds(pair * 2 * DH + 2 * HEADS * DH, 2 * DH)]).then_inc(wv_loaded, 16)

            def load_o(pair):
                act.dma_start(w_o[:, :], a["w_out"][ds(pair * 128, 128), :]).then_inc(wo_loaded, 16)

            def high_qk_weights(par, turn):
                act.wait_ge(qk_loaded[par], 32 * turn)
                for s in range(2):
                    last = af(qk_h[par][:, s, :, :],
                              qk_raw[par][:, s, :].rearrange("p (a d) -> p a d", a=1).to_broadcast([C, 2, DH]), ACT.Copy)
                last.then_inc(qkw_hi, 1)

            def high_v_weights(pair):
                act.wait_ge(wv_loaded, 16 * (pair + 1))
                af(wv_h[:, :], wv_raw[:, :], ACT.Copy).then_inc(vw_hi, 1)

            def high_qk(head, par, i):
                c, s = i // 2, i % 2
                act.wait_ge(proj_ps, 8 * head + i + 1)
                dst = (qa if s == 0 else ka)[par]
                af(dst[:, c * CH:c * CH + CH], ps[:, QK_BANKS[i % 4], :], ACT.Copy,
                   scale=SCORE_SCALE if s == 0 else 1.0).then_inc(hi_done, 1)

            def high_v(pair):
                for b in range(4):
                    act.wait_ge(v_ps, 4 * pair + b + 1)
                    for h in range(2):
                        last = af(v_h[:, h, 4 * b:4 * b + 4, 0:DH],
                                  ps[:, 2 + b % 2, :].rearrange("p (t h d) -> p h t d", t=4, h=2)[:, h, :, :], ACT.Copy)
                    last.then_inc(v_hi, 1)

            def turn_maxima(head, wait_store=True):
                act.wait_ge(mt_ps, head + 1)
                if wait_store:
                    act.wait_ge(m_loaded, 16 * head)
                af(m_t[:, :], ps[0:NT, 7, 0:128], ACT.Copy).then_inc(mt_done, 1)

            def row_sums(head, c):
                act.wait_ge(pv_done, GROUPS * (NC * head + c + 1))
                af(l_row[DH:DH + 1, ds(c * CH, CH)], ps[DH:DH + 1, 6, :], ACT.Copy).then_inc(l_done, 1)

            def main_chunk(head, c, first):
                n0 = GROUPS * (NC * head + c)
                for g in range(GROUPS):
                    if g == PV_LAG and not first:
                        row_sums(head, c - 1)
                    act.wait_ge(st_ps, n0 + g + 1)
                    if not first or g >= 2:
                        act.wait_ge(pl_even, n0 + g - 1)
                        act.wait_ge(pl_odd, n0 + g - 1)
                    af(p_raw[:, g % 2, :, :], ps[:, 2 * (g % 2):2 * (g % 2) + 2, :], ACT.Exp).then_inc(exp_done, 1)
                    act.wait_ge(exp_done, n0 + g + 1)
                    if not first or g >= 4:
                        act.wait_ge(pv_done, n0 + g - 3)
                    af(p_h[:, g % 4, :, :], p_raw[:, g % 2, :, :], ACT.Copy).then_inc(ph_done, 1)

            def window(pair, par, with_next, project, with_v):
                head = 2 * pair + par
                later = not (isinstance(pair, int) and pair == 0)
                if project:
                    act.wait_ge(qkw_lo, head + 1)
                    load_qk(head + 2, par)
                    if par == 0:
                        act.wait_ge(vw_lo, pair + 1)
                        load_v(pair + 1)
                if par == 0 and later:
                    act.wait_ge(out_ps, PRIME + NC * (pair - 1))
                    load_o(pair - 1)
                main_chunk(head, 0, True)
                if project:
                    high_qk_weights(par, pair + 2)
                    if par == 0:
                        high_v_weights(pair + 1)
                if later or par == 1:
                    act.wait_ge(l_stored, 16 * head)
                with act.Fori(1, NC) as c:
                    main_chunk(head, c, False)
                if project:
                    for i in range(4):
                        high_qk(head + 2, par, i)
                if with_next:
                    turn_maxima(head + 1)
                if project:
                    for i in range(4, 6):
                        high_qk(head + 2, par, i)
                row_sums(head, NC - 1)
                if project:
                    for i in range(6, 8):
                        high_qk(head + 2, par, i)
                if with_v:
                    high_v(pair + 1)

            QK_BANKS = (4, 5, 0, 1)

            def attention():
                high_parts(3)
                for head in range(2):
                    high_qk_weights(head, 1)
                high_v_weights(0)
                for head in range(2):
                    for i in range(8):
                        high_qk(head, head, i)
                high_v(0)
                turn_maxima(0, False)
                window(0, 0, True, True, False)
                window(0, 1, True, True, True)
                with act.Fori(1, PAIRS - 1) as pair:
                    window(pair, 0, True, True, False)
                    window(pair, 1, True, True, True)
                window(PAIRS - 1, 0, True, False, False)
                window(PAIRS - 1, 1, False, False, False)
                act.wait_ge(out_ps, PRIME + NC * (PAIRS - 1))
                load_o(PAIRS - 1)

            layer_norm(0)
            moe(0)
            layer_norm(1)
            rwkv()
            layer_norm(2)
            moe(1)
            layer_norm(3)
            act.wait_ge(x_ready, PRIME + NC * 3)
            load_qk(0, 0)
            load_qk(1, 1)
            load_v(0)
            quant_ffn(0)
            layer_norm(4)
            rms_norm()
            attention()
            layer_norm(5)
            quant_ffn(1)

        @block.vector
        def _(dve):
            tt = nc.vector.tensor_tensor
            stt = nc.vector.scalar_tensor_tensor
            ts = nc.vector.tensor_scalar
            for primed in (x_ready, h_done, h_relu, w2_done, y_gate, s_max, o_scaled, f_prod, f_down, o_done, l_done, out_ps, out_add):
                nc.vector.sem_inc(primed, PRIME)
            steps = [0]

            def step(ins):
                steps[0] += 1
                ins.then_inc(dve_step, 1)
                dve.wait_ge(dve_step, steps[0])

            def layer_norm(k):
                for c in range(NC):
                    dve.wait_ge(ln_mean, NC * k + c + 1)
                    tt(cen[:, chunk(c)], x[:, chunk(c)], ps[:, c, :], ALU.subtract).then_inc(ln_cen, 1)
                dve.wait_ge(ln_var, k + 1)
                ts(ln_v[:, :], ps[:, 4, 0:NT], LN_EPS, None, ALU.add).then_inc(ln_add, 1)
                dve.wait_ge(ln_std, k + 1)
                nc.vector.reciprocal(ln_r[:, :], ln_s[:, :]).then_inc(ln_rec, 1)
                for c in range(NC):
                    dve.wait_ge(ln_bc, NC * k + c + 1)
                    dve.wait_ge(ln_cen, NC * (k + 1))
                    tt(xn[:, chunk(c)], cen[:, chunk(c)], ps[:, c, :], ALU.mult).then_inc(ln_out, 1)

            def low_parts(j):
                for c in range(NC):
                    dve.wait_ge(xh_done, NC * j + c + 1)
                    tt(x_l[:, chunk(c)], xn[:, chunk(c)], x_h[:, chunk(c)].bitcast(fp32), ALU.subtract).then_inc(xl_done, 1)

            def bc(col):
                return col.rearrange("p (t a) -> p t a", a=1).to_broadcast([128, NT, E])

            def pick(src, hot, top):
                step(nc.vector.tensor_reduce(rt[:, top, :], src[:, :, :], AX.X, ALU.max))
                step(tt(eq[:, :, :], src[:, :, :], bc(rt[:, top, :]), ALU.is_equal))
                step(tt(eq[:, :, :], eq[:, :, :],
                        rank[:, :].rearrange("p (a e) -> p a e", a=1).to_broadcast([128, NT, E]), ALU.mult))
                step(nc.vector.tensor_reduce(rt[:, 7, :], eq[:, :, :], AX.X, ALU.max))
                step(tt(hot[:, :, :], eq[:, :, :], bc(rt[:, 7, :]), ALU.is_equal))

            def moe(k):
                if k == 0:
                    dve.wait_ge(const_ready, CONST)
                    dve.wait_ge(small_loaded, 16 * 6)
                dve.wait_ge(rt_logits, k + 1)
                step(tt(lg[:, :, :], ps[:, 5, 0:NT * E].rearrange("p (t e) -> p t e", e=E),
                        rb[:, :].rearrange("p (a e) -> p a e", a=1).to_broadcast([128, NT, E]), ALU.add))
                pick(lg, best, 0)
                step(stt(lg2[:, :, :], best[:, :, :], EXCLUDE, lg[:, :, :], ALU.mult, ALU.add))
                pick(lg2, second, 1)
                tt(rt[:, 2, :], rt[:, 1, :], rt[:, 0, :], ALU.subtract).then_inc(rt_diff, 1)
                dve.wait_ge(rt_exp, k + 1)
                step(ts(rt[:, 4, :], rt[:, 3, :], 1.0, None, ALU.add))
                step(nc.vector.reciprocal(rt[:, 5, :], rt[:, 4, :]))
                step(tt(rt[:, 6, :], rt[:, 3, :], rt[:, 5, :], ALU.mult))
                step(tt(best[:, :, :], best[:, :, :], bc(rt[:, 5, :]), ALU.mult))
                step(tt(second[:, :, :], second[:, :, :], bc(rt[:, 6, :]), ALU.mult))
                tt(gates[:, :, :], best[:, :, :], second[:, :, :], ALU.add).then_inc(rt_gates, 1)
                low_parts(k)
                if k == 0:
                    dve.wait_ge(w_hi, 1)
                    tt(w1_l[:, :, :], w1_raw, w1_h[:, :, :].bitcast(fp32), ALU.subtract).then_inc(w_lo, 1)
                    dve.wait_ge(w_hi, 2)
                    tt(w2_l[:, :, :, :].rearrange("p e a n -> p (e a n)"), w2_raw.rearrange("p e a n -> p (e a n)"),
                       w2_h[:, :, :, :].bitcast(fp32).rearrange("p e a n -> p (e a n)"), ALU.subtract).then_inc(w_lo, 1)
                with dve.Fori(0, NC) as c:
                    at = k * NC + c

                    def low(u):
                        tt(h_l[:, u % 4, :], h_raw[:, u % 4, :], h_h[:, u % 4, :].bitcast(fp32), ALU.subtract).then_inc(h_done, 1)

                    def add_expert(e):
                        n = at * E + e
                        dve.wait_ge(w2_done, PRIME + at * UNITS + HT0 * (e + 1))
                        dve.wait_ge(g_loaded[e], 16 * (at + 1))
                        stt(y_gated[:, e % 2, :], ps[:, 4 + e % 2, :], b2[:, e:e + 1], g_bc[:, e, :],
                            ALU.add, ALU.mult).then_inc(y_gate, 1)

                    def finish_expert(e):
                        n = at * E + e
                        dve.wait_ge(y_gate, PRIME + n + 1)
                        if e > 0:
                            dve.wait_ge(y_add, at * (E - 1) + e)
                        stt(x[:, ds(c * CH, CH)], y_gated[:, e % 2, :], 0.5, x[:, ds(c * CH, CH)],
                            ALU.mult, ALU.add).then_inc(y_add if e < E - 1 else x_ready, 1)
                    for u in range(0, UNITS, 2):
                        v = u + 1
                        dve.wait_ge(h_relu, PRIME + at * UNITS + v + 1)
                        dve.wait_ge(w2_done, PRIME + at * UNITS + max(v - 3, 0))
                        nc.vector.tensor_copy(h_h[:, v % 4, :], h_raw[:, v % 4, :]).then_inc(h_hi2, 1)
                        dve.wait_ge(h_hi, at * (UNITS // 2) + u // 2 + 1)
                        low(u)
                        dve.wait_ge(h_hi2, at * (UNITS // 2) + u // 2 + 1)
                        low(v)
                        done = v - LAG - HT0
                        if done >= 0 and (done + 1) % HT0 == 2:
                            add_expert(done // HT0)
                        if done >= 0 and (done + 1) % HT0 == 0:
                            finish_expert(done // HT0)
                    add_expert(E - 2)
                    finish_expert(E - 2)
                    add_expert(E - 1)
                    finish_expert(E - 1)

            def rwkv():
                s = lambda n, off=0: big[:, n, off:off + T]
                dve.wait_ge(ln_out, NC * 2)
                step(tt(s(0), xn, xprev, ALU.subtract))
                for j in range(3):
                    stt(s(2 + j), s(0), mix[:, j:j + 1], xprev, ALU.mult, ALU.add).then_inc(mixed, 1)
                dve.wait_ge(mixed, 3)
                dve.wait_ge(act_step, 1)
                step(ts(decay[:, 1:2], decay[:, 0:1], -1.0, None, ALU.mult))
                w = decay[:, 1:2]
                k_, v_, r_ = s(5), s(6), s(7)
                p, p_next = s(0), s(0, 1)
                step(nc.vector.memset(big[:, 0, 0:1], NO_STATE))
                dve.wait_ge(kvr_done, NC)
                step(nc.vector.tensor_tensor_scan(p_next, w.to_broadcast([C, T]), k_, NO_STATE, ALU.add, ALU.max))
                stt(s(1, 1), p, w, p_next, ALU.add, ALU.subtract).then_inc(wkv_arg, 1)
                dve.wait_ge(kvr_ps, NC * 3)
                tt(s(2, 1), k_, p_next, ALU.subtract).then_inc(wkv_arg, 1)
                step(stt(s(3, 1), k_, mix[:, 4:5], p, ALU.add, ALU.max))
                tt(s(4, 1), p, s(3, 1), ALU.subtract).then_inc(wkv_arg, 1)
                dve.wait_ge(wkv_arg, 3)
                stt(s(3, 1), k_, mix[:, 4:5], s(3, 1), ALU.add, ALU.subtract).then_inc(wkv_arg, 1)
                f1, f2, e1, e2 = s(1, 1), s(2, 1), s(4, 1), s(3, 1)
                dve.wait_ge(wkv_arg, 4)
                step(nc.vector.memset(big[:, 0, 0:1], 0.0))
                dve.wait_ge(wkv_exp, 2)
                step(nc.vector.tensor_tensor_scan(s(0, 1), f1, f2, 0.0, ALU.mult, ALU.add))
                dve.wait_ge(kvr_done, NC * 2)
                step(tt(f2, f2, v_, ALU.mult))
                step(nc.vector.memset(big[:, 5, 0:1], 0.0))
                step(nc.vector.tensor_tensor_scan(s(5, 1), f1, f2, 0.0, ALU.mult, ALU.add))
                dve.wait_ge(wkv_exp, 4)
                step(tt(s(0), e1, s(0), ALU.mult))
                step(tt(s(0), s(0), e2, ALU.add))
                step(tt(s(5), e1, s(5), ALU.mult))
                step(tt(e2, e2, v_, ALU.mult))
                step(tt(s(5), s(5), e2, ALU.add))
                step(nc.vector.reciprocal(s(1), s(0)))
                dve.wait_ge(kvr_done, NC * 3)
                step(tt(s(5), s(5), s(1), ALU.mult))
                tt(s(2), s(5), r_, ALU.mult).then_inc(wkv_out, 1)
                for c in range(NC):
                    dve.wait_ge(o_ps, c + 1)
                    tt(x[:, chunk(c)], x[:, chunk(c)], ps[:, 4 + c, :], ALU.add).then_inc(x_ready, 1)

            def quant_ffn(k, before):
                low_parts(2 * k + 2)
                with dve.Fori(0, NC) as c:
                    at = k * NC + c
                    for ht in range(HT1):
                        n = at * HT1 + ht
                        dve.wait_ge(f_sigmoid, n + 1)
                        stt(f_sig[:, ht, :], ps[:, 2 * ht, :], QUANT_SCALE, f_sig[:, ht, :], ALU.mult, ALU.mult).then_inc(f_silu, 1)
                        dve.wait_ge(f_silu, n + 1)
                        if ht == 0:
                            dve.wait_ge(f_down, PRIME + at)
                        stt(f_hid[:, ht, :], ps[:, 2 * ht + 1, :], QUANT_SCALE, f_sig[:, ht, :], ALU.mult, ALU.mult).then_inc(f_prod, 1)
                    dve.wait_ge(f_down, PRIME + at + 1)
                    stt(x[:, ds(c * CH, CH)], ps[:, 6, :], 0.5 * QUANT_SCALE, x[:, ds(c * CH, CH)],
                        ALU.mult, ALU.add).then_inc(x_ready, 1)

            def rms_norm():
                dve.wait_ge(rms_sum, 1)
                ts(ln_v[:, :], ps[:, 4, 0:NT], float(C), None, ALU.mult).then_inc(rms_add, 1)
                dve.wait_ge(rms_std, 1)
                step(ts(ln_s[:, :], ln_s[:, :], RMS_EPS, None, ALU.max))
                step(nc.vector.reciprocal(ln_r[:, :], ln_s[:, :]))
                ts(ln_r[:, :], ln_r[:, :], float(C) ** 0.5, None, ALU.mult).then_inc(rms_rec, 1)
                for c in range(NC):
                    dve.wait_ge(rms_bc, c + 1)
                    stt(xn[:, chunk(c)], xn[:, chunk(c)], gamma1[:, 0:1], ps[:, c, :], ALU.mult, ALU.mult).then_inc(rms_out, 1)

            def low_qk_weights(par, head):
                dve.wait_ge(qkw_hi, head + 1)
                for s in range(2):
                    last = tt(qk_l[par][:, s, :, :],
                              qk_raw[par][:, s, :].rearrange("p (a d) -> p a d", a=1).to_broadcast([C, 2, DH]),
                              qk_h[par][:, s, :, :].bitcast(fp32), ALU.subtract)
                last.then_inc(qkw_lo, 1)

            def low_v_weights(pair):
                dve.wait_ge(vw_hi, pair + 1)
                tt(wv_l[:, :], wv_raw[:, :], wv_h[:, :].bitcast(fp32), ALU.subtract).then_inc(vw_lo, 1)

            QK_BANKS = (4, 5, 0, 1)

            def low_qk(head, par, i):
                c, s = i // 2, i % 2
                cols = slice(c * CH, c * CH + CH)
                bank = QK_BANKS[i % 4]
                dve.wait_ge(hi_done, 8 * head + i + 1)
                if s == 0:
                    stt(qb[par][0:DH, cols], ps[0:DH, bank, :], SCORE_SCALE, qa[par][0:DH, cols].bitcast(fp32),
                        ALU.mult, ALU.subtract).then_inc(lo_done, 1)
                else:
                    tt(ka[par][DH:128, cols], ps[DH:128, bank, :], ka[par][DH:128, cols].bitcast(fp32),
                       ALU.subtract).then_inc(lo_done, 1)
                    nc.vector.tensor_copy(kb[par][0:DH, cols], ka[par][0:DH, cols].bitcast(fp32)).then_inc(kb_done, 1)

            def low_v(pair):
                for b in range(4):
                    dve.wait_ge(v_hi, 4 * pair + b + 1)
                    for h in range(2):
                        last = tt(v_l[:, h, 4 * b:4 * b + 4, 0:DH],
                                  ps[:, 2 + b % 2, :].rearrange("p (t h d) -> p h t d", t=4, h=2)[:, h, :, :],
                                  v_h[:, h, 4 * b:4 * b + 4, 0:DH].bitcast(fp32), ALU.subtract)
                    last.then_inc(v_lo, 1)

            def maximum(head, c, it):
                dve.wait_ge(s_ps, NC * NT * head + NT * c + it + 1)
                nc.vector.tensor_reduce(m_part[:, ds(c, 1), it:it + 1].rearrange("p a t -> p (a t)"),
                                        ps[:, 4 + it % 2, :], AX.X, ALU.max).then_inc(s_max, 1)

            def maxima_end(head, par):
                dve.wait_ge(s_max, PRIME + NC * NT * (head + 1))
                nc.vector.tensor_reduce(m_col[par][:, :], m_part[:, :, :].rearrange("p c t -> p t c"),
                                        AX.X, ALU.max, negate=True).then_inc(m_ready, 1)

            def outputs(head, par, c, later):
                rows = slice(par * DH, par * DH + DH)
                if later:
                    dve.wait_ge(o_scaled, PRIME + NC * (head - 1))
                dve.wait_ge(pv_done, GROUPS * (NC * head + c + 1))
                nc.vector.tensor_copy(o_raw[rows, ds(c * CH, CH)], ps[0:DH, 6, :]).then_inc(o_done, 1)

            def invert(head, par):
                dve.wait_ge(l_loaded, 16 * (head + 1))
                nc.vector.reciprocal(r_col[:, par, :], l_col[:, par, :]).then_inc(r_ready, 1)

            def add_out(pair, c, bank):
                dve.wait_ge(out_ps, PRIME + NC * pair + c + 1)
                tt(x[:, ds(c * CH, CH)], x[:, ds(c * CH, CH)], ps[:, bank, :], ALU.add).then_inc(out_add, 1)

            def main_chunk(pair, par, c, first, with_next, with_out, invert_before):
                head = 2 * pair + par
                later = not (isinstance(pair, int) and pair == 0)
                n0 = GROUPS * (NC * head + c)
                for g in range(GROUPS):
                    if g == PV_LAG and not first:
                        outputs(head, par, c - 1, later)
                    if with_next:
                        maximum(head + 1, c, 2 * g)
                        maximum(head + 1, c, 2 * g + 1)
                    dve.wait_ge(ph_done, n0 + g + 1)
                    if not first or g >= 4:
                        dve.wait_ge(pv_done, n0 + g - 3)
                    tt(p_l[:, g % 4, 0, :], p_raw[:, g % 2, 0, :], p_h[:, g % 4, 0, :].bitcast(fp32),
                       ALU.subtract).then_inc(pl_even, 1)
                    if g == 4 and first and invert_before:
                        invert(head - 1, 1 - par)
                    if g == 6 and with_out:
                        add_out(pair - 1, c, 7)

            def window(pair, par, with_next, project, with_v):
                head = 2 * pair + par
                later = not (isinstance(pair, int) and pair == 0)
                with_out = par == 1 and later
                main_chunk(pair, par, 0, True, with_next, with_out, later or par == 1)
                if project:
                    low_qk_weights(par, head + 2)
                    if par == 0:
                        low_v_weights(pair + 1)
                with dve.Fori(1, NC) as c:
                    main_chunk(pair, par, c, False, with_next, with_out, False)
                if with_next:
                    maxima_end(head + 1, 1 - par)
                if project:
                    for i in range(6):
                        low_qk(head + 2, par, i)
                outputs(head, par, NC - 1, later)
                if project:
                    for i in range(6, 8):
                        low_qk(head + 2, par, i)
                if with_v:
                    low_v(pair + 1)

            def attention():
                low_parts(3)
                for head in range(2):
                    low_qk_weights(head, head)
                low_v_weights(0)
                for head in range(2):
                    for i in range(8):
                        low_qk(head, head, i)
                low_v(0)
                with dve.Fori(0, NC) as c:
                    for it in range(NT):
                        maximum(0, c, it)
                maxima_end(0, 0)
                window(0, 0, True, True, False)
                window(0, 1, True, True, True)
                with dve.Fori(1, PAIRS - 1) as pair:
                    window(pair, 0, True, True, False)
                    window(pair, 1, True, True, True)
                window(PAIRS - 1, 0, True, False, False)
                window(PAIRS - 1, 1, False, False, False)
                invert(HEADS - 1, 1)
                dve.wait_ge(out_add, PRIME + NC * (PAIRS - 1))
                for c in range(NC):
                    dve.wait_ge(out_ps, PRIME + NC * (PAIRS - 1) + c + 1)
                    tt(x[:, chunk(c)], x[:, chunk(c)], ps[:, c, :], ALU.add).then_inc(x_ready, 1)

            layer_norm(0)
            moe(0)
            layer_norm(1)
            rwkv()
            layer_norm(2)
            moe(1)
            layer_norm(3)
            dve.wait_ge(l1_loaded, 16 * 3)
            nc.vector.tensor_copy(wgu[:, :, :], wgu_i[:, :, :]).then_inc(dequantised, 1)
            nc.vector.tensor_copy(wd[:, :, :], wd_i[:, :, :]).then_inc(dequantised, 1)
            step(ts(gamma1[:, :], gamma1[:, :], 1.0, None, ALU.add))
            quant_ffn(0, 3)
            layer_norm(4)
            rms_norm()
            attention()
            layer_norm(5)
            quant_ffn(1, 5)


def kernel(**inputs):
    import numpy as np
    import concourse.bacc as bacc
    from concourse.bass_utils import run_bass_kernel_spmd

    g = {n: np.asarray(v) for n, v in inputs.items()}
    laid = {
        "xT": g["L0_attn_x"][0].T,
        "router_w": g["L0_ffn_router_w"],
        "router_b": g["L0_ffn_router_b"],
        "w1T": g["L0_ffn_w1"].transpose(1, 0, 2),
        "b1T": g["L0_ffn_b1"].reshape(E, HT0, 128).transpose(2, 0, 1),
        "w2T": g["L0_ffn_w2"].reshape(E, HT0, 128, C).transpose(2, 0, 1, 3),
        "b2T": g["L0_ffn_b2"].T,
        "rwkv_wT": np.stack([g["L0_attn_" + n].T for n in ("Wk", "Wv", "Wr", "Wo")], axis=1),
        "mix": np.stack([g["L0_attn_" + n].reshape(C) for n in
                         ("time_mix_k", "time_mix_v", "time_mix_r", "time_decay", "time_first")], axis=1),
        "gamma": g["L1_attn_gamma"].reshape(C, 1),
        "w_qkv": g["L1_attn_w_qkv"],
        "w_out": g["L1_attn_w_out"],
        "w_gate_upT": np.stack([g["L1_ffn_w_gate"].T, g["L1_ffn_w_up"].T], axis=1),
        "w_downT": g["L1_ffn_w_down"].T.reshape(HT1, 128, C).transpose(1, 0, 2),
    }
    nc = bacc.Bacc("TRN2", target_bir_lowering=False, num_devices=1)
    arrays, aps = {}, {}
    for name, v in laid.items():
        v = np.ascontiguousarray(v)
        arrays[f"in_{name}"] = v
        aps[name] = nc.dram_tensor(f"in_{name}", v.shape, mybir.dt.from_np(v.dtype), kind="ExternalInput").ap()
    out = nc.dram_tensor("out_xT", (C, T), fp32, kind="ExternalOutput").ap()
    g_scratch = nc.dram_tensor("g_scratch", (2, E, T), fp32, kind="Internal").ap()
    l_scratch = nc.dram_tensor("l_scratch", (HEADS, T), fp32, kind="Internal").ap()
    r_scratch = nc.dram_tensor("r_scratch", (HEADS, T), fp32, kind="Internal").ap()
    macaron_kernel(nc, aps, out, g_scratch, l_scratch, r_scratch)
    r = run_bass_kernel_spmd(nc, [arrays], core_ids=[0])
    return np.ascontiguousarray(r.results[0]["out_xT"].T).reshape(1, T, C)
```

```python
import concourse.bass as bass
from concourse import mybir
from concourse.alu_op_type import AluOpType as ALU
from contextlib import ExitStack

fp32 = mybir.dt.float32
fp32r = mybir.dt.float32r
int32 = mybir.dt.int32
ACT = mybir.ActivationFunctionType
AX = mybir.AxisListType
ds = bass.ds

C = 128
T = 2048
CH = 512
NC = T // CH
NT = T // 128
TPC = CH // 128
E, H0 = 8, 512
HT0 = H0 // 128
UNITS = E * HT0
HEADS, DH = 16, 64
PAIRS = HEADS // 2
H1 = 384
HT1 = H1 // 128
GROUPS = NT // 2
LN_EPS = 1e-5
RMS_EPS = 1e-12
QUANT_SCALE = 1.0 / 127.0
SCORE_SCALE = DH ** -0.5
NO_STATE = -1e38
EXCLUDE = -3.0e38
LAG = 4
PV_LAG = 2
END_GROUPS = (4, 5, 7)
PRIME = 1
PROJECTED = {(3, 3): 0, (3, 4): 1, (3, 6): 2}
TURN_BANK, END_BANK = 4, 5
POOL_GROUPS = (2, 4)
SCALE_GROUP = 3
V_STEPS = NT // 2
V_AT = ({(1, 3): 0, (1, 5): 1, (1, 6): 2, (2, 3): 3, (2, 5): 4, (2, 6): 5}, {(0, 3): 6, (0, 4): 7})
V_SPLIT = ((0, 3), (1, 0))
OUT_GROUP = (6, 6, 6, 7)
MAXIMA_TILES = ((0, 2, 2, 3, 2, 2, 3, 2), (2,) * 8, (2,) * 8, (3, 3, 3, 2, 2, 2, 1, 0))
WKV_SLOTS = (1, 2, 4, 3)




def macaron_kernel(nc, a, out, g_scratch, l_scratch, r_scratch):
    ctx = ExitStack()
    with ctx:
        def sb(name, shape, dt=fp32, where=ctx):
            return where.enter_context(nc.sbuf_tensor(name, shape, dt))

        def sem(name):
            return ctx.enter_context(nc.semaphore(name))

        x = sb("x", [C, T])
        xnp = sb("xnp", [C, T + 1])
        xn = xnp[:, 1:T + 1]
        xprev = xnp[:, 0:T]
        x_h = sb("x_h", [C, T], fp32r)
        x_l = sb("x_l", [C, T], fp32r)
        cen = sb("cen", [C, T])
        sqr = sb("sqr", [C, T])
        ident = sb("ident", [128, 128])
        inv_c = sb("inv_c", [128, 128])
        ln_s = sb("ln_s", [128, NT])
        eps = sb("eps", [128, 1])
        ln_r = sb("ln_r", [128, NT])
        gamma1 = sb("gamma1", [C, 1])

        one = ExitStack()
        big = sb("big", [C, 8, T + 8], where=one)
        w1_h = sb("w1_h", [C, E, H0], fp32r, one)
        w1_l = sb("w1_l", [C, E, H0], fp32r, one)
        w2_h = sb("w2_h", [128, E, HT0, C], fp32r, one)
        w2_l = sb("w2_l", [128, E, HT0, C], fp32r, one)
        b1 = sb("b1", [128, E, HT0], where=one)
        b2 = sb("b2", [C, E], where=one)
        rw = sb("rw", [C, E], where=one)
        rb = sb("rb", [128, E], where=one)
        rank = sb("rank", [128, E], where=one)
        lg = sb("lg", [128, NT, E], where=one)
        lg2 = sb("lg2", [128, NT, E], where=one)
        eq = sb("eq", [128, NT, E], where=one)
        best = sb("best", [128, NT, E], where=one)
        second = sb("second", [128, NT, E], where=one)
        gates = sb("gates", [128, NT, E], where=one)
        rt = sb("rt", [128, 8, NT], where=one)
        h_h = sb("h_h", [128, 4, CH], fp32r, one)
        h_l = sb("h_l", [128, 4, CH], fp32r, one)
        rwkv_w = sb("rwkv_w", [C, 4, C], where=one)
        mix = sb("mix", [C, 5], where=one)
        decay = sb("decay", [C, 2], where=one)
        one.close()
        flat = big[:, :, :].rearrange("p a n -> p (a n)")
        S1 = T + 8
        g_bc = flat[:, 0:E * CH].rearrange("p (e n) -> p e n", e=E)
        w1_raw = flat[:, 2 * S1:2 * S1 + E * H0].rearrange("p (e n) -> p e n", e=E)
        w2_raw = flat[:, 4 * S1:4 * S1 + E * H0].rearrange("p (e a n) -> p e a n", e=E, a=HT0)
        h_raw = big[:, 6, 0:4 * CH].rearrange("p (a n) -> p a n", a=4)
        g_t = big[0:E, 7, 0:T]
        y_gated = sqr[:, 0:2 * CH].rearrange("p (a n) -> p a n", a=2)

        two = ExitStack()
        wgu = sb("wgu", [C, 2, H1], fp32r, two)
        wd = sb("wd", [128, HT1, C], fp32r, two)
        ka = [sb(f"ka{i}", [128, T], fp32r, two) for i in range(2)]
        kb = [sb(f"kb{i}", [DH + 1, T], fp32r, two) for i in range(2)]
        qa = [sb(f"qa{i}", [128, T], fp32r, two) for i in range(2)]
        qb = [sb(f"qb{i}", [DH + 1, T], fp32r, two) for i in range(2)]
        v_h = sb("v_h", [128, 2, NT, DH + 1], fp32r, two)
        v_l = sb("v_l", [128, 2, NT, DH + 1], fp32r, two)
        p_raw = sb("p_raw", [128, 4, 2, CH], where=two)
        p_h = sb("p_h", [128, 4, 2, CH], fp32r, two)
        p_l = sb("p_l", [128, 4, 2, CH], fp32r, two)
        qk_raw = [sb(f"qk_raw{i}", [C, 2, DH], where=two) for i in range(2)]
        qk_h = [sb(f"qk_h{i}", [C, 2, DH], fp32r, two) for i in range(2)]
        qk_l = [sb(f"qk_l{i}", [C, 2, DH], fp32r, two) for i in range(2)]
        wv_raw = sb("wv_raw", [C, 2 * DH], where=two)
        wv_hl = sb("wv_hl", [C, 2, 2 * DH], fp32r, two)
        v_raw = sb("v_raw", [128, NT, 2 * DH], where=two)
        w_o = sb("w_o", [128, C], where=two)
        w_o_end = sb("w_o_end", [128, C], where=two)
        m_part = sb("m_part", [128, NC, NT], where=two)
        m_col = [sb(f"m_col{i}", [128, NT], where=two) for i in range(2)]
        m_t = sb("m_t", [NT, 128], fp32r, two)
        l_row = sb("l_row", [DH + 1, T], where=two)
        l_col = sb("l_col", [128, 2, NT], where=two)
        r_col = sb("r_col", [128, 2, NT], where=two)
        two.close()
        int_flat = v_raw[:, :, :].rearrange("p a n -> p (a n)").bitcast(int32)
        wgu_i = int_flat[:, 0:2 * H1].rearrange("p (g n) -> p g n", g=2)
        wd_i = int_flat[:, 2 * H1:2 * H1 + HT1 * C].rearrange("p (a n) -> p a n", a=HT1)
        o_raw, o_nrm, r_bc = cen, sqr, xn
        f_sig = p_raw[:, 0:2, :, :].rearrange("p a b n -> p (a b) n")
        f_hid = cen[:, 0:HT1 * CH].rearrange("p (a n) -> p a n", a=HT1)
        f_h = p_h[:, 0:2, :, :].rearrange("p a b n -> p (a b) n")
        f_l = p_l[:, 0:2, :, :].rearrange("p a b n -> p (a b) n")

        ps = ctx.enter_context(nc.psum_tensor("ps", [128, 8, CH], fp32))

        x_loaded = [sem(f"x_loaded{c}") for c in range(NC)]
        small_loaded = sem("small_loaded")
        w1_loaded, w2_loaded = sem("w1_loaded"), sem("w2_loaded")
        l1_loaded = sem("l1_loaded")
        const_step, const_ready = sem("const_step"), sem("const_ready")
        l1_const, dequantised = sem("l1_const"), sem("dequantised")
        x_ready = sem("x_ready")
        dve_step = sem("dve_step")
        act_step = sem("act_step")
        wkv_prod, wkv_den, wkv_inv = sem("wkv_prod"), sem("wkv_den"), sem("wkv_inv")
        ln_mean, ln_cen, ln_sq, ln_var = sem("ln_mean"), sem("ln_cen"), sem("ln_sq"), sem("ln_var")
        ln_std, ln_rec, ln_bc, ln_out = sem("ln_std"), sem("ln_rec"), sem("ln_bc"), sem("ln_out")
        xh_done, xl_done = sem("xh_done"), sem("xl_done")
        w_hi, w_lo = sem("w_hi"), sem("w_lo")
        rt_logits, rt_diff, rt_exp, rt_gates = sem("rt_logits"), sem("rt_diff"), sem("rt_exp"), sem("rt_gates")
        gt_ps, gt_done, g_stored = sem("gt_ps"), sem("gt_done"), sem("g_stored")
        g_loaded = [sem(f"g_loaded{e}") for e in range(E)]
        h_ps, h_relu, h_hi, h_hi2, h_done = sem("h_ps"), sem("h_relu"), sem("h_hi"), sem("h_hi2"), sem("h_done")
        w2_done, y_gate, y_add = sem("w2_done"), sem("y_gate"), sem("y_add")
        mixed, kvr_ps, kvr_done, wkv_arg, wkv_exp = sem("mixed"), sem("kvr_ps"), sem("kvr_done"), sem("wkv_arg"), sem("wkv_exp")
        wkv_out, o_ps = sem("wkv_out"), sem("o_ps")
        f_ps, f_sigmoid, f_silu, f_prod, f_hi, f_lo, f_down = (
            sem("f_ps"), sem("f_sigmoid"), sem("f_silu"), sem("f_prod"), sem("f_hi"), sem("f_lo"), sem("f_down"))
        rms_sq, rms_sum, rms_std, rms_rec, rms_bc, rms_out = (
            sem("rms_sq"), sem("rms_sum"), sem("rms_std"), sem("rms_rec"), sem("rms_bc"), sem("rms_out"))
        qk_loaded = [sem("qk_loaded0"), sem("qk_loaded1")]
        wv_loaded, wo_loaded = sem("wv_loaded"), sem("wo_loaded")
        qkw_hi, qkw_lo, vw_hi, vw_lo = sem("qkw_hi"), sem("qkw_lo"), sem("vw_hi"), sem("vw_lo")
        v_ps, v_sum, v_hi, v_lo = sem("v_ps"), sem("v_sum"), sem("v_hi"), sem("v_lo")
        proj_ps, hi_done, lo_done, kb_done = sem("proj_ps"), sem("hi_done"), sem("lo_done"), sem("kb_done")
        m_ready, mt_ps, mt_done, m_loaded = sem("m_ready"), sem("mt_ps"), sem("mt_done"), sem("m_loaded")
        st_ps, exp_done, ph_done, pl_even, pl_odd, pv_done = (
            sem("st_ps"), sem("exp_done"), sem("ph_done"), sem("pl_even"), sem("pl_odd"), sem("pv_done"))
        s_ps, s_max = sem("s_ps"), sem("s_max")
        o_done, l_done = sem("o_done"), sem("l_done")
        l_stored, l_loaded, r_ready, r_stored, r_loaded, o_scaled = (
            sem("l_stored"), sem("l_loaded"), sem("r_ready"), sem("r_stored"), sem("r_loaded"), sem("o_scaled"))
        out_ps, out_add = sem("out_ps"), sem("out_add")
        end_w, end_l, end_r, end_o, end_ps = sem("end_w"), sem("end_l"), sem("end_r"), sem("end_o"), sem("end_ps")
        stored = sem("stored")

        block = ctx.enter_context(nc.Block())

        def chunk(c):
            return ds(c * CH, CH)

        def sums_bank(c):
            return 6 + c % 2

        def spare_bank(c):
            return 6 + (c + 1) % 2

        def first_of_all(pair, par, c=0):
            return isinstance(pair, int) and pair == 0 and par == 0 and c == 0

        def low_parts_done(eng, head, c, g):
            if g < 0:
                c, g = c - 1, g + GROUPS
            own = GROUPS - len(POOL_GROUPS)
            eng.wait_ge(pl_even, own * (NC * head + c) + sum(i not in POOL_GROUPS for i in range(g + 1)))
            eng.wait_ge(pl_odd, GROUPS * (NC * head + c) + g + 1)

        def wait_x(eng, k, c):
            if k == 0:
                eng.wait_ge(x_loaded[c], 16)
            else:
                eng.wait_ge(x_ready, PRIME + NC * (k - 1) + c + 1)

        @block.sync
        def _(sp):
            for c in range(NC):
                sp.dma_start(x[:, chunk(c)], a["xT"][:, chunk(c)]).then_inc(x_loaded[c], 16)
            sp.dma_start(rw[:, :], a["router_w"]).then_inc(small_loaded, 16)
            sp.dma_start(rb[:, :], a["router_b"].rearrange("(a e) -> a e", a=1).to_broadcast([128, E])).then_inc(small_loaded, 16)
            sp.dma_start(b1[:, :, :], a["b1T"]).then_inc(small_loaded, 16)
            sp.dma_start(b2[:, :], a["b2T"]).then_inc(small_loaded, 16)
            sp.dma_start(rwkv_w[:, :, :], a["rwkv_wT"]).then_inc(small_loaded, 16)
            sp.dma_start(mix[:, :], a["mix"]).then_inc(small_loaded, 16)
            sp.dma_start(w1_raw, a["w1T"]).then_inc(w1_loaded, 16)
            sp.dma_start(w2_raw, a["w2T"]).then_inc(w2_loaded, 16)
            sp.dma_start(gamma1[:, :], a["gamma"]).then_inc(l1_loaded, 16)

            def gates_everywhere(k):
                sp.wait_ge(gt_done, NC * (k + 1))
                sp.dma_start(g_scratch[k, :, :], g_t).then_inc(g_stored, 16)
                sp.wait_ge(g_stored, 16 * (k + 1))
                for e in range(E):
                    if k > 0:
                        sp.wait_ge(y_gate, PRIME + E * NC * k)
                    sp.dma_start(g_bc[:, e, :], g_scratch[k, e:e + 1, 0:CH].to_broadcast([128, CH])).then_inc(g_loaded[e], 16)
                with sp.Fori(1, NC) as c:
                    for e in range(E):
                        sp.wait_ge(y_gate, PRIME + E * (NC * k + c - 1) + e + 1)
                        sp.dma_start(g_bc[:, e, :], g_scratch[k, e:e + 1, ds(c * CH, CH)].to_broadcast([128, CH])).then_inc(g_loaded[e], 16)

            gates_everywhere(0)
            gates_everywhere(1)
            sp.wait_ge(x_ready, PRIME + NC * 3)
            sp.dma_start(wgu_i, a["w_gate_upT"]).then_inc(l1_loaded, 16)
            sp.dma_start(wd_i, a["w_downT"]).then_inc(l1_loaded, 16)

            def maxima_row(head, par):
                sp.wait_ge(mt_done, head + 1)
                sp.dma_start(qb[par][DH:DH + 1, :].bitcast(fp32), m_t[:, :].bitcast(fp32)).then_inc(m_loaded, 16)

            def normalise(head, par):
                sp.wait_ge(l_done, PRIME + NC * (head + 1))
                sp.dma_start(l_scratch[ds(head, 1), :], l_row[DH:DH + 1, :]).then_inc(l_stored, 16)
                sp.wait_ge(l_stored, 16 * (head + 1))
                sp.dma_start(l_col[:, par, :], l_scratch[ds(head, 1), :].rearrange("a (p t) -> (a p) t", p=128)).then_inc(l_loaded, 16)
                sp.wait_ge(r_ready, head + 1)
                sp.dma_start(r_scratch[ds(head, 1), :].rearrange("a (p t) -> (a p) t", p=128), r_col[:, par, :]).then_inc(r_stored, 16)
                sp.wait_ge(r_stored, 16 * (head + 1))
                sp.wait_ge(o_scaled, PRIME + NC * head)
                sp.dma_start(r_bc[par * DH:par * DH + DH, :],
                             r_scratch[ds(head, 1), :].to_broadcast([DH, T])).then_inc(r_loaded, 16)

            def load_qk(head, par):
                for s in range(2):
                    sp.dma_start(qk_raw[par][:, s, :],
                                  a["w_qkv"][:, ds(head * DH + s * HEADS * DH, DH)]).then_inc(qk_loaded[par], 16)

            def load_v(pair):
                sp.dma_start(wv_raw[:, :], a["w_qkv"][:, ds(pair * 2 * DH + 2 * HEADS * DH, 2 * DH)]).then_inc(wv_loaded, 16)

            def load_o(pair):
                sp.dma_start(w_o[:, :], a["w_out"][ds(pair * 128, 128), :]).then_inc(wo_loaded, 16)

            def weights(pair, par, of_qkv, of_out):
                head = 2 * pair + par
                if of_qkv:
                    sp.wait_ge(qkw_lo, head + 1)
                    load_qk(head + 2, par)
                    if par == 0:
                        sp.wait_ge(vw_lo, pair + 1)
                        load_v(pair + 1)
                if of_out:
                    sp.wait_ge(out_ps, PRIME + NC * (pair - 1))
                    load_o(pair - 1)

            load_qk(0, 0)
            load_qk(1, 1)
            load_v(0)
            sp.dma_start(w_o_end[:, :], a["w_out"][(PAIRS - 1) * 128:PAIRS * 128, :]).then_inc(end_w, 16)
            maxima_row(0, 0)
            weights(0, 0, True, False)
            maxima_row(1, 1)
            with sp.Fori(0, PAIRS - 2) as pair:
                weights(pair, 1, True, False)
                normalise(2 * pair, 0)
                maxima_row(2 * pair + 2, 0)
                weights(pair + 1, 0, True, True)
                normalise(2 * pair + 1, 1)
                maxima_row(2 * pair + 3, 1)
            weights(PAIRS - 2, 1, True, False)
            normalise(HEADS - 4, 0)
            maxima_row(HEADS - 2, 0)
            weights(PAIRS - 1, 0, False, True)
            normalise(HEADS - 3, 1)
            maxima_row(HEADS - 1, 1)
            normalise(HEADS - 2, 0)
            for c in range(NC):
                sp.wait_ge(x_ready, PRIME + NC * 5 + c + 1)
                sp.dma_start(out[:, chunk(c)], x[:, chunk(c)]).then_inc(stored, 16)
            sp.wait_ge(stored, 16 * NC)

        @block.gpsimd
        def _(pool):
            nc.gpsimd.memset(ident[:, :], 0.0).then_inc(const_step, 1)
            nc.gpsimd.memset(inv_c[:, :], 1.0 / C).then_inc(const_ready, 1)
            nc.gpsimd.memset(xnp[:, 0:1], 0.0).then_inc(const_ready, 1)
            nc.gpsimd.memset(eps[:, :], LN_EPS).then_inc(const_ready, 1)
            for e in range(E):
                nc.gpsimd.memset(rank[:, e:e + 1], float(E - e)).then_inc(const_ready, 1)
            pool.wait_ge(const_step, 1)
            nc.gpsimd.affine_select(out=ident[:, :], in_=ident[:, :], compare_op=ALU.not_equal, fill=1.0,
                                    base=0, pattern=[[-1, 128]], channel_multiplier=1).then_inc(const_ready, 1)
            pool.wait_ge(w_hi, 2)
            nc.gpsimd.tensor_tensor(w2_l[:, :, :, :].rearrange("p e a n -> p (e a n)"), w2_raw.rearrange("p e a n -> p (e a n)"),
                                    w2_h[:, :, :, :].bitcast(fp32).rearrange("p e a n -> p (e a n)"), ALU.subtract).then_inc(w_lo, 1)
            pool.wait_ge(kvr_done, NC * 2)
            for n, slot, product in ((2, 2, cen), (4, 3, sqr)):
                pool.wait_ge(wkv_exp, n)
                nc.gpsimd.tensor_tensor(product[:, :], big[:, slot, 1:T + 1], big[:, 6, 0:T], ALU.mult).then_inc(wkv_prod, 1)
            pool.wait_ge(x_ready, PRIME + NC * 3)
            for i in range(2):
                nc.gpsimd.memset(kb[i][DH:DH + 1, :].bitcast(fp32), 1.0).then_inc(l1_const, 1)
            pool.wait_ge(l1_const, 2)
            nc.gpsimd.memset(v_h[:, :, :, DH:DH + 1].bitcast(fp32), 1.0).then_inc(l1_const, 1)
            nc.gpsimd.memset(v_l[:, :, :, DH:DH + 1].bitcast(fp32), 0.0).then_inc(l1_const, 1)

            def quant_ffn(k):
                for c in range(NC):
                    at = k * NC + c
                    for ht in range(HT1):
                        pool.wait_ge(f_hi, at * HT1 + ht + 1)
                        pool.wait_ge(f_down, PRIME + at)
                        nc.gpsimd.tensor_tensor(f_l[:, ht, :], f_hid[:, ht, :], f_h[:, ht, :].bitcast(fp32),
                                                ALU.subtract).then_inc(f_lo, 1)

            def low_part(head, c, g, start):
                n = GROUPS * (NC * head + c) + g
                pool.wait_ge(ph_done, n + 1)
                if not start or g >= 4:
                    pool.wait_ge(pv_done, n - 3)
                tiles = slice(0 if g in POOL_GROUPS else 1, 2)
                nc.gpsimd.tensor_tensor(p_l[:, g % 4, tiles, :], p_raw[:, g % 4, tiles, :], p_h[:, g % 4, tiles, :].bitcast(fp32),
                                        ALU.subtract).then_inc(pl_odd, 1)

            def low_v(head, par, low_parts):
                pool.wait_ge(v_hi, head + 1)
                pool.wait_ge(pl_odd, low_parts)
                nc.gpsimd.tensor_tensor(v_l[:, par, :, 0:DH], v_raw[:, :, par * DH:par * DH + DH],
                                        v_h[:, par, :, 0:DH].bitcast(fp32), ALU.subtract).then_inc(v_lo, 1)

            def scale(head, par, piece, low_parts, wait_out=None):
                rows = slice(par * DH, par * DH + DH)
                pool.wait_ge(r_loaded, 16 * (head + 1))
                pool.wait_ge(o_done, PRIME + NC * (head + 1))
                if wait_out is not None:
                    pool.wait_ge(out_ps, PRIME + wait_out)
                pool.wait_ge(pl_odd, low_parts)
                nc.gpsimd.tensor_tensor(o_nrm[rows, ds(piece * CH, CH)], o_raw[rows, ds(piece * CH, CH)],
                                        r_bc[rows, ds(piece * CH, CH)], ALU.mult).then_inc(o_scaled, 1)
                pool.wait_ge(o_scaled, PRIME + NC * head + piece + 1)

            def window(pair, par, scale_before, project):
                head = 2 * pair + par
                for g in range(GROUPS):
                    low_part(head, 0, g, first_of_all(pair, par))
                    if par == 0 and (0, g) == V_SPLIT[0]:
                        low_v(head + 1, 1, GROUPS * NC * head + g + 1)

                later = not (isinstance(pair, int) and pair == 0)

                def piece(q, low_parts):
                    scale(head - 1, 1 - par, q, low_parts, NC * (pair - 1) + q + 1 if par == 1 and later else None)
                for c in range(1, NC):
                    for g in range(GROUPS):
                        low_part(head, c, g, False)
                        if par == 1 and project and (c, g) == V_SPLIT[1]:
                            low_v(head + 1, 0, GROUPS * (NC * head + c) + g + 1)
                        if g == SCALE_GROUP and scale_before:
                            piece(c - 1, GROUPS * (NC * head + c) + g + 1)
                if scale_before:
                    piece(NC - 1, GROUPS * NC * (head + 1))

            def attention():
                pool.wait_ge(v_hi, 1)
                nc.gpsimd.tensor_tensor(v_l[:, 0, :, 0:DH], v_raw[:, :, 0:DH], v_h[:, 0, :, 0:DH].bitcast(fp32),
                                        ALU.subtract).then_inc(v_lo, 1)
                window(0, 0, False, True)
                window(0, 1, True, True)
                with pool.Fori(1, PAIRS - 1) as pair:
                    window(pair, 0, True, True)
                    window(pair, 1, True, True)
                window(PAIRS - 1, 0, True, False)
                window(PAIRS - 1, 1, True, False)

            quant_ffn(0)
            attention()
            quant_ffn(1)
        CONST = 3 + E + 1
        L1_CONST = 4

        @block.tensor
        def _(pe):
            mm = nc.tensor.matmul

            def variances(src_ready, count, done, c):
                pe.wait_ge(src_ready, count)
                for t in range(TPC):
                    tile = slice(c * CH + t * 128, c * CH + t * 128 + 128)
                    last = mm(ps[:, 4 + c, t:t + 1], sqr[:, tile], inv_c[:, 0:1], start=True, stop=True)
                last.then_inc(done, 1)

            def spread(src_ready, count, done, c):
                pe.wait_ge(src_ready, count)
                for t in range(TPC):
                    last = mm(ps[:, c, t * 128:t * 128 + 128],
                              ln_r[:, TPC * c + t:TPC * c + t + 1].to_broadcast([128, 128]), ident[:, :], start=True, stop=True)
                last.then_inc(done, 1)

            def layer_norm(k):
                if k == 0:
                    pe.wait_ge(const_ready, CONST)
                for c in range(NC):
                    wait_x(pe, k, c)
                    mm(ps[:, c, :], inv_c[:, :], x[:, chunk(c)], start=True, stop=True).then_inc(ln_mean, 1)
                for c in range(NC + 1):
                    if c < NC:
                        variances(ln_sq, NC * k + c + 1, ln_var, c)
                    if c > 0:
                        spread(ln_rec, NC * k + c, ln_bc, c - 1)

            def split_product(o, w_hi_, w_lo_, x_hi_, x_lo_, start, stop):
                mm(o, w_lo_, x_hi_, start=start, stop=False)
                mm(o, w_hi_, x_hi_, start=False, stop=False)
                return mm(o, w_hi_, x_lo_, start=False, stop=stop)

            def moe(k):
                pe.wait_ge(ln_out, NC * (k * 2 + 1))
                pe.wait_ge(small_loaded, 16 * 6)
                for t in range(NT):
                    last = mm(ps[:, 5, t * E:t * E + E], xn[:, t * 128:t * 128 + 128], rw[:, :], start=True, stop=True)
                last.then_inc(rt_logits, 1)
                pe.wait_ge(rt_gates, k + 1)
                for c in range(NC):
                    for t in range(TPC):
                        last = mm(ps[0:E, c, t * 128:t * 128 + 128], gates[:, TPC * c + t, :], ident[:, :], start=True, stop=True)
                    last.then_inc(gt_ps, 1)
                pe.wait_ge(gt_done, NC * (k + 1))
                pe.wait_ge(xl_done, NC * (k + 1))
                if k == 0:
                    pe.wait_ge(w_lo, 2)
                with pe.Fori(0, NC) as c:
                    at = (k * NC + c)

                    def second_product(u):
                        e, ht = u // HT0, u % HT0
                        if ht == 0:
                            pe.wait_ge(y_gate, PRIME + at * E + max(e - 1, 0))
                        pe.wait_ge(h_done, PRIME + at * UNITS + u + 1)
                        split_product(ps[:, 4 + e % 2, :], w2_h[:, e, ht, :], w2_l[:, e, ht, :], h_h[:, u % 4, :], h_l[:, u % 4, :],
                                      ht == 0, ht == HT0 - 1).then_inc(w2_done, 1)
                    for u in range(UNITS):
                        e, ht = u // HT0, u % HT0
                        pe.wait_ge(h_relu, PRIME + at * UNITS + max(u - 3, 0))
                        cols = slice(ht * 128, ht * 128 + 128)
                        split_product(ps[:, u % 4, :], w1_h[:, e, cols], w1_l[:, e, cols], x_h[:, chunk(c)], x_l[:, chunk(c)],
                                      True, True).then_inc(h_ps, 1)
                        if u >= LAG:
                            second_product(u - LAG)
                    for u in range(UNITS - LAG, UNITS):
                        second_product(u)

            def rwkv():
                for j in range(3):
                    for c in range(NC):
                        pe.wait_ge(mixed, c + 1 if j == 0 else NC + j)
                        if j == 2:
                            pe.wait_ge(kvr_done, c + 1)
                        mm(ps[:, (4 if j == 1 else 0) + c, :], rwkv_w[:, j, :], big[:, 2 + j, ds(c * CH, CH)],
                           start=True, stop=True).then_inc(kvr_ps, 1)
                for c in range(NC):
                    pe.wait_ge(wkv_out, c + 1)
                    mm(ps[:, 4 + c, :], rwkv_w[:, 3, :], big[:, 2, ds(c * CH, CH)], start=True, stop=True).then_inc(o_ps, 1)

            def quant_ffn(k, before):
                def gate_and_up(c):
                    pe.wait_ge(xl_done, NC * (2 * k + 2) + c + 1)
                    for ht in range(HT1):
                        pe.wait_ge(f_prod, PRIME + max((k * NC + c - 1) * HT1 + ht + 1, 0))
                        for g in range(2):
                            w = wgu[:, g, ht * 128:ht * 128 + 128]
                            mm(ps[:, 2 * ht + g, :], w, x_h[:, chunk(c)], start=True, stop=False)
                            last = mm(ps[:, 2 * ht + g, :], w, x_l[:, chunk(c)], start=False, stop=True)
                        last.then_inc(f_ps, 1)

                def down(c):
                    pe.wait_ge(x_ready, PRIME + NC * before + max(c - 1, 0))
                    for ht in range(HT1):
                        pe.wait_ge(f_lo, (k * NC + c) * HT1 + ht + 1)
                        mm(ps[:, 6 + c % 2, :], wd[:, ht, :], f_h[:, ht, :], start=(ht == 0), stop=False)
                        last = mm(ps[:, 6 + c % 2, :], wd[:, ht, :], f_l[:, ht, :], start=False, stop=(ht == HT1 - 1))
                    last.then_inc(f_down, 1)

                pe.wait_ge(dequantised, 2)
                gate_and_up(0)
                for c in range(1, NC):
                    gate_and_up(c)
                    down(c - 1)
                down(NC - 1)

            def rms_norm():
                for c in range(NC + 1):
                    if c < NC:
                        variances(rms_sq, c + 1, rms_sum, c)
                    if c > 0:
                        spread(rms_rec, c, rms_bc, c - 1)

            def project_qk(par, c, bank):
                w_hi_ = qk_h[par][:, :, :].rearrange("p a d -> p (a d)")
                w_lo_ = qk_l[par][:, :, :].rearrange("p a d -> p (a d)")
                split_product(ps[:, bank, :], w_hi_, w_lo_, x_h[:, chunk(c)], x_l[:, chunk(c)], True, True).then_inc(proj_ps, 1)

            def project_v(b, bank):
                for t in range(2):
                    tile = slice((2 * b + t) * 128, (2 * b + t) * 128 + 128)
                    o = ps[:, bank, t * 256:t * 256 + 256]
                    w = wv_hl[:, :, :].rearrange("p a d -> p (a d)")
                    mm(o, x_h[:, tile], w, start=True, stop=False)
                    last = mm(o, x_l[:, tile], w, start=False, stop=True)
                last.then_inc(v_ps, 1)

            def score_tile(head, par, c, it):
                if it < 2:
                    pe.wait_ge(s_max, PRIME + NC * NT * head + NT * c)
                else:
                    pe.wait_ge(s_max, PRIME + NC * NT * head + NT * c + it - 1)
                mm(ps[:, 4 + it % 2, :], qa[par][:, it * 128:it * 128 + 128], ka[par][:, ds(c * CH, CH)],
                   start=True, stop=True).then_inc(s_ps, 1)

            def turn_maxima(head, par):
                pe.wait_ge(m_ready, head + 1)
                mm(ps[0:NT, TURN_BANK, 0:128], m_col[par][:, :], ident[:, :], start=True, stop=True).then_inc(mt_ps, 1)

            def values(head, par, c, g):
                low_parts_done(pe, head, c, g)
                for j in range(2):
                    jt = 2 * g + j
                    last = split_product(ps[0:DH + 1, sums_bank(c), :], v_h[:, par, jt, :], v_l[:, par, jt, :],
                                         p_h[:, g % 4, j, :], p_l[:, g % 4, j, :], jt == 0, jt == NT - 1)
                last.then_inc(pv_done, 1)

            def scores_t(par, c, g):
                for j in range(2):
                    jt = 2 * g + j
                    st = ps[:, 2 * (g % 2) + j, :]
                    mm(st, ka[par][:, jt * 128:jt * 128 + 128], qa[par][:, ds(c * CH, CH)], start=True, stop=False)
                    last = mm(st, kb[par][:, jt * 128:jt * 128 + 128], qb[par][:, ds(c * CH, CH)], start=False, stop=True)
                last.then_inc(st_ps, 1)

            def project_out(c, bank):
                mm(ps[:, bank, :], w_o[:, :], o_nrm[:, chunk(c)], start=True, stop=True).then_inc(out_ps, 1)

            def main_chunk(pair, par, c, with_next, project, with_out):
                head = 2 * pair + par
                n0 = GROUPS * (NC * head + c)
                first, start = c == 0, first_of_all(pair, par, c)
                later = not (isinstance(pair, int) and pair == 0)

                def read(at, g_at):
                    qk = [n for (k, g), n in PROJECTED.items() if (k, g) < (at, g_at)]
                    if project and qk:
                        pe.wait_ge(hi_done, 12 * (head + 2) + 3 * max(qk) + 3)
                        pe.wait_ge(lo_done, 8 * (head + 2) + 2 * max(qk) + 2)
                    steps = [b for (k, g), b in V_AT[par].items() if (k, g) < (at, g_at)]
                    if project and steps:
                        pe.wait_ge(v_sum, V_STEPS * (pair + 1) + max(steps) + 1)
                    if with_out and g_at > OUT_GROUP[at]:
                        pe.wait_ge(out_add, PRIME + NC * (pair - 1) + at + 1)

                def spare_free(g):
                    pe.wait_ge(o_done, PRIME + NC * head + c)
                    pe.wait_ge(l_done, PRIME + NC * head + c)
                    read(c, g)

                tiles = iter(range(NT))

                def next_score_tile():
                    it = next(tiles)
                    if first and it % TPC == 0:
                        pe.wait_ge(lo_done, 8 * (head + 1) + 2 * (it // TPC) + 2)
                        pe.wait_ge(hi_done, 12 * (head + 1) + 3 * (it // TPC) + 3)
                    if first and it == 1:
                        pe.wait_ge(hi_done, 12 * (head + 2))
                        pe.wait_ge(lo_done, 8 * (head + 2))
                    score_tile(head + 1, 1 - par, c, it)

                for g in range(GROUPS):
                    if with_next and (c, g) == (NC - 1, GROUPS - 1):
                        turn_maxima(head + 1, 1 - par)
                    if not start or g >= 2:
                        pe.wait_ge(exp_done, n0 + g - 1)
                    elif g == 0:
                        pe.wait_ge(v_sum, V_STEPS)
                    scores_t(par, c, g)
                    if with_next and first and g == 0:
                        before = 0
                    else:
                        before = min(1, MAXIMA_TILES[c][g])
                    if with_next:
                        for _ in range(before):
                            next_score_tile()
                    if g < PV_LAG and not first:
                        values(head, par, c - 1, GROUPS - PV_LAG + g)
                    if g < PV_LAG and first and not start:
                        values(head - 1, 1 - par, NC - 1, GROUPS - PV_LAG + g)
                    if g == PV_LAG:
                        if not start:
                            pe.wait_ge(o_done, PRIME + NC * head + c - 1)
                            pe.wait_ge(l_done, PRIME + NC * head + c - 1)
                        if not first:
                            read(c - 1, GROUPS)
                        else:
                            pe.wait_ge(v_lo, head + 1)
                            if par == 0 and later:
                                pe.wait_ge(out_add, PRIME + NC * (pair - 1))
                    if g >= PV_LAG:
                        values(head, par, c, g - PV_LAG)
                    if with_next:
                        for _ in range(MAXIMA_TILES[c][g] - before):
                            next_score_tile()
                    n = PROJECTED.get((c, g)) if project else None
                    if n is not None:
                        if n == 0:
                            pe.wait_ge(qkw_lo, head + 3)
                        spare_free(g)
                        project_qk(par, n, spare_bank(c))
                    b = V_AT[par].get((c, g)) if project else None
                    if b is not None:
                        pe.wait_ge(vw_lo, pair + 2)
                        spare_free(g)
                        project_v(b, spare_bank(c))
                    if with_out and g == OUT_GROUP[c]:
                        if first:
                            pe.wait_ge(o_scaled, PRIME + NC * head - NC)
                            pe.wait_ge(wo_loaded, 16 * pair)
                        spare_free(g)
                        project_out(c, spare_bank(c))
                    if not with_next and par == 1 and c > 0 and g == END_GROUPS[0]:
                        end_spread(c - 1)
                    if not with_next and par == 1 and c > 0 and g == END_GROUPS[2]:
                        end_out(c - 1)

            def end_spread(c):
                pe.wait_ge(l_done, PRIME + NC * (HEADS - 1) + c + 1)
                if c > 0:
                    pe.wait_ge(end_r, c)
                mm(ps[:, 4, :], kb[0][DH:DH + 1, 0:128].bitcast(fp32), l_row[DH:DH + 1, chunk(c)], start=True, stop=True).then_inc(end_l, 1)

            def end_out(c):
                if c == 0:
                    pe.wait_ge(end_w, 16)
                pe.wait_ge(o_scaled, PRIME + NC * (HEADS - 2) + c + 1)
                pe.wait_ge(end_o, c + 1)
                if c > 0:
                    pe.wait_ge(x_ready, PRIME + NC * 4 + c)
                mm(ps[:, 5, :], w_o_end[:, :], o_nrm[:, chunk(c)], start=True, stop=True).then_inc(end_ps, 1)

            def window(pair, par, with_next, project):
                head = 2 * pair + par
                with_out = par == 1 and not (isinstance(pair, int) and pair == 0)
                pe.wait_ge(m_loaded, 16 * (head + 1))
                pe.wait_ge(kb_done, NC * (head + 1))
                for c in range(NC):
                    main_chunk(pair, par, c, with_next, project, with_out)
                if project:
                    project_qk(par, NC - 1, END_BANK)

            def attention():
                pe.wait_ge(xl_done, NC * 4)
                pe.wait_ge(l1_const, L1_CONST)
                for head in range(2):
                    pe.wait_ge(qkw_lo, head + 1)
                    for c in range(NC):
                        project_qk(head, c, NC * head + c)
                pe.wait_ge(lo_done, 8)
                pe.wait_ge(hi_done, 12)
                pe.wait_ge(vw_lo, 1)
                for b in range(V_STEPS):
                    if b >= 4:
                        pe.wait_ge(v_sum, b - 3)
                    project_v(b, b % 4)
                pe.wait_ge(lo_done, 16)
                pe.wait_ge(hi_done, 24)
                for it in range(NT):
                    if it >= 2:
                        pe.wait_ge(s_max, PRIME + NC * (it - 1))
                    if it == 1:
                        pe.wait_ge(v_sum, V_STEPS)
                    for c in range(NC):
                        mm(ps[:, 4 * ((it + 1) % 2) + c, :], qa[0][:, it * 128:it * 128 + 128], ka[0][:, chunk(c)],
                           start=True, stop=True).then_inc(s_ps, 1)
                turn_maxima(0, 0)
                window(0, 0, True, True)
                window(0, 1, True, True)
                with pe.Fori(1, PAIRS - 1) as pair:
                    window(pair, 0, True, True)
                    window(pair, 1, True, True)
                window(PAIRS - 1, 0, True, False)
                window(PAIRS - 1, 1, False, False)
                for g in (GROUPS - 2, GROUPS - 1):
                    values(HEADS - 1, 1, NC - 1, g)
                end_spread(NC - 1)
                end_out(NC - 1)

            layer_norm(0)
            moe(0)
            layer_norm(1)
            rwkv()
            layer_norm(2)
            moe(1)
            layer_norm(3)
            quant_ffn(0, 3)
            layer_norm(4)
            rms_norm()
            attention()
            layer_norm(5)
            quant_ffn(1, 5)

        @block.scalar
        def _(act):
            af = nc.scalar.activation

            def layer_norm(k):
                for c in range(NC):
                    act.wait_ge(ln_cen, NC * k + c + 1)
                    af(sqr[:, chunk(c)], cen[:, chunk(c)], ACT.Square).then_inc(ln_sq, 1)
                if k == 0:
                    act.wait_ge(const_ready, CONST)
                for c in range(NC):
                    act.wait_ge(ln_var, NC * k + c + 1)
                    af(ln_s[:, TPC * c:TPC * c + TPC], ps[:, 4 + c, 0:TPC], ACT.Sqrt, bias=eps[:, 0:1]).then_inc(ln_std, 1)

            def high_parts(j):
                for c in range(NC):
                    if j == 3:
                        act.wait_ge(rms_out, c + 1)
                    else:
                        act.wait_ge(ln_out, NC * (0, 2, 3, 0, 5)[j] + c + 1)
                    af(x_h[:, chunk(c)], xn[:, chunk(c)], ACT.Copy).then_inc(xh_done, 1)

            def split_weights():
                act.wait_ge(w1_loaded, 16)
                af(w1_h[:, :, :], w1_raw, ACT.Copy).then_inc(w_hi, 1)
                act.wait_ge(w2_loaded, 16)
                af(w2_h[:, :, :, :].rearrange("p e a n -> p (e a n)"), w2_raw.rearrange("p e a n -> p (e a n)"),
                   ACT.Copy).then_inc(w_hi, 1)

            def moe(k):
                high_parts(k)
                if k == 0:
                    split_weights()
                act.wait_ge(rt_diff, k + 1)
                af(rt[:, 3, :], rt[:, 2, :], ACT.Exp).then_inc(rt_exp, 1)
                for c in range(NC):
                    act.wait_ge(gt_ps, NC * k + c + 1)
                    af(g_t[:, chunk(c)], ps[0:E, c, :], ACT.Copy).then_inc(gt_done, 1)
                with act.Fori(0, NC) as c:
                    at = k * NC + c
                    for u in range(UNITS):
                        e, ht = u // HT0, u % HT0
                        act.wait_ge(h_ps, at * UNITS + u + 1)
                        act.wait_ge(h_done, PRIME + at * UNITS + max(u - 3, 0))
                        af(h_raw[:, u % 4, :], ps[:, u % 4, :], ACT.Relu, bias=b1[:, e, ht:ht + 1]).then_inc(h_relu, 1)
                        if u % 2 == 1:
                            act.wait_ge(h_relu, PRIME + at * UNITS + u)
                            act.wait_ge(w2_done, PRIME + at * UNITS + max(u - 4, 0))
                            af(h_h[:, (u - 1) % 4, :], h_raw[:, (u - 1) % 4, :], ACT.Copy).then_inc(h_hi, 1)

            def rwkv():
                act.wait_ge(small_loaded, 16 * 6)
                af(decay[:, 0:1], mix[:, 3:4], ACT.Exp).then_inc(act_step, 1)
                for j in range(3):
                    for c in range(NC):
                        act.wait_ge(kvr_ps, NC * j + c + 1)
                        src = ps[:, (4 if j == 1 else 0) + c, :]
                        af(big[:, 5 + j, ds(c * CH, CH)], src, ACT.Copy if j < 2 else ACT.Sigmoid).then_inc(kvr_done, 1)
                for n in range(4):
                    act.wait_ge(wkv_arg, n + 1)
                    s = WKV_SLOTS[n]
                    af(big[:, s, 1:T + 1], big[:, s, 1:T + 1], ACT.Exp).then_inc(wkv_exp, 1)
                act.wait_ge(wkv_prod, 1)
                for c in range(NC):
                    act.wait_ge(wkv_den, c + 1)
                    af(big[:, 2, chunk(c)], big[:, 0, chunk(c)], ACT.Ln).then_inc(act_step, 1)
                for c in range(NC):
                    act.wait_ge(act_step, c + 2)
                    af(big[:, 2, chunk(c)], big[:, 2, chunk(c)], ACT.Exp, scale=-1.0).then_inc(wkv_inv, 1)

            def quant_ffn(k):
                high_parts(2 * k + 2)
                for c in range(NC):
                    at = k * NC + c
                    for ht in range(HT1):
                        act.wait_ge(f_ps, at * HT1 + ht + 1)
                        af(f_sig[:, ht, :], ps[:, 2 * ht, :], ACT.Sigmoid, scale=QUANT_SCALE).then_inc(f_sigmoid, 1)
                    for ht in range(HT1):
                        act.wait_ge(f_prod, PRIME + at * HT1 + ht + 1)
                        act.wait_ge(f_down, PRIME + at)
                        af(f_h[:, ht, :], f_hid[:, ht, :], ACT.Copy).then_inc(f_hi, 1)

            def rms_norm():
                for c in range(NC):
                    act.wait_ge(ln_out, NC * 4 + c + 1)
                    af(sqr[:, chunk(c)], xn[:, chunk(c)], ACT.Square).then_inc(rms_sq, 1)
                for c in range(NC):
                    act.wait_ge(rms_sum, c + 1)
                    af(ln_s[:, TPC * c:TPC * c + TPC], ps[:, 4 + c, 0:TPC], ACT.Sqrt, scale=float(C)).then_inc(rms_std, 1)

            def high_qk_weights(par, turn):
                act.wait_ge(qk_loaded[par], 32 * turn)
                af(qk_h[par][:, :, :], qk_raw[par][:, :, :], ACT.Copy).then_inc(qkw_hi, 1)

            def high_v_weights(pair):
                act.wait_ge(wv_loaded, 16 * (pair + 1))
                af(wv_hl[:, 0, :], wv_raw[:, :], ACT.Copy).then_inc(vw_hi, 1)

            def high_qk(head, par, c, bank):
                act.wait_ge(proj_ps, NC * head + c + 1)
                af(qa[par][0:DH, chunk(c)], ps[0:DH, bank, :], ACT.Copy, scale=SCORE_SCALE).then_inc(hi_done, 1)
                af(ka[par][DH:128, chunk(c)], ps[DH:128, bank, :], ACT.Copy).then_inc(hi_done, 1)
                act.wait_ge(hi_done, 12 * head + 3 * c + 1)
                af(qa[par][DH:128, chunk(c)], qa[par][0:DH, chunk(c)].bitcast(fp32), ACT.Copy).then_inc(hi_done, 1)

            def high_v(pair, head, par):
                act.wait_ge(v_sum, V_STEPS * (pair + 1))
                if par == 1 or not (isinstance(head, int) and head == 0):
                    act.wait_ge(pv_done, GROUPS * NC * (head - 1))
                af(v_h[:, par, :, 0:DH], v_raw[:, :, par * DH:par * DH + DH], ACT.Copy).then_inc(v_hi, 1)

            def turn_maxima(head, wait_store=True):
                act.wait_ge(mt_ps, head + 1)
                if wait_store:
                    act.wait_ge(m_loaded, 16 * head)
                af(m_t[:, :], ps[0:NT, TURN_BANK, 0:128], ACT.Copy).then_inc(mt_done, 1)

            def row_sums(head, c):
                act.wait_ge(pv_done, GROUPS * (NC * head + c + 1))
                af(l_row[DH:DH + 1, chunk(c)], ps[DH:DH + 1, sums_bank(c), :], ACT.Copy).then_inc(l_done, 1)

            def main_chunk(pair, par, c, with_next, project):
                head = 2 * pair + par
                n0 = GROUPS * (NC * head + c)
                start = first_of_all(pair, par, c)
                for g in range(GROUPS):
                    if with_next and (c, g) == (NC - 1, GROUPS - 1):
                        turn_maxima(head + 1)
                    act.wait_ge(st_ps, n0 + g + 1)
                    if not start or g >= 4:
                        low_parts_done(act, head, c, g - 4)
                    af(p_raw[:, g % 4, :, :], ps[:, 2 * (g % 2):2 * (g % 2) + 2, :], ACT.Exp).then_inc(exp_done, 1)
                    act.wait_ge(exp_done, n0 + g + 1)
                    if not start or g >= 4:
                        act.wait_ge(pv_done, n0 + g - 3)
                    af(p_h[:, g % 4, :, :], p_raw[:, g % 4, :, :], ACT.Copy).then_inc(ph_done, 1)
                    if g == PV_LAG and not start:
                        row_sums(head if c > 0 else head - 1, (c - 1) % NC)
                    n = PROJECTED.get((c, g)) if project else None
                    if n is not None:
                        high_qk(head + 2, par, n, spare_bank(c))
                    if (c, g) == V_SPLIT[par] and (par == 0 or project):
                        high_v(pair + par, head + 1, 1 - par)

            def window(pair, par, with_next, project):
                head = 2 * pair + par
                later = not (isinstance(pair, int) and pair == 0)
                main_chunk(pair, par, 0, with_next, project)
                if project:
                    high_qk_weights(par, pair + 2)
                    if par == 0:
                        high_v_weights(pair + 1)
                if later or par == 1:
                    act.wait_ge(l_stored, 16 * head)
                for c in range(1, NC):
                    main_chunk(pair, par, c, with_next, project)
                if project:
                    high_qk(head + 2, par, NC - 1, END_BANK)

            def attention():
                high_parts(3)
                for head in range(2):
                    high_qk_weights(head, 1)
                high_v_weights(0)
                for head in range(2):
                    for c in range(NC):
                        high_qk(head, head, c, NC * head + c)
                high_v(0, 0, 0)
                turn_maxima(0, False)
                window(0, 0, True, True)
                window(0, 1, True, True)
                with act.Fori(1, PAIRS - 1) as pair:
                    window(pair, 0, True, True)
                    window(pair, 1, True, True)
                window(PAIRS - 1, 0, True, False)
                window(PAIRS - 1, 1, False, False)
                row_sums(HEADS - 1, NC - 1)

            layer_norm(0)
            moe(0)
            layer_norm(1)
            rwkv()
            layer_norm(2)
            moe(1)
            layer_norm(3)
            quant_ffn(0)
            layer_norm(4)
            rms_norm()
            attention()
            layer_norm(5)
            quant_ffn(1)

        @block.vector
        def _(dve):
            tt = nc.vector.tensor_tensor
            stt = nc.vector.scalar_tensor_tensor
            ts = nc.vector.tensor_scalar
            for primed in (x_ready, h_done, h_relu, w2_done, y_gate, s_max, o_scaled, f_prod, f_down, o_done, l_done, out_ps, out_add):
                nc.vector.sem_inc(primed, PRIME)
            steps = [0]

            def step(ins):
                steps[0] += 1
                ins.then_inc(dve_step, 1)
                dve.wait_ge(dve_step, steps[0])

            def layer_norm(k):
                for c in range(NC):
                    dve.wait_ge(ln_mean, NC * k + c + 1)
                    tt(cen[:, chunk(c)], x[:, chunk(c)], ps[:, c, :], ALU.subtract).then_inc(ln_cen, 1)
                for c in range(NC + 1):
                    if c < NC:
                        tiles = slice(TPC * c, TPC * c + TPC)
                        dve.wait_ge(ln_std, NC * k + c + 1)
                        nc.vector.reciprocal(ln_r[:, tiles], ln_s[:, tiles]).then_inc(ln_rec, 1)
                    if c > 0:
                        dve.wait_ge(ln_bc, NC * k + c)
                        dve.wait_ge(ln_cen, NC * k + c)
                        tt(xn[:, chunk(c - 1)], cen[:, chunk(c - 1)], ps[:, c - 1, :], ALU.mult).then_inc(ln_out, 1)

            def low_parts(j):
                for c in range(NC):
                    dve.wait_ge(xh_done, NC * j + c + 1)
                    tt(x_l[:, chunk(c)], xn[:, chunk(c)], x_h[:, chunk(c)].bitcast(fp32), ALU.subtract).then_inc(xl_done, 1)

            def bc(col):
                return col.rearrange("p (t a) -> p t a", a=1).to_broadcast([128, NT, E])

            def pick(src, hot, top):
                step(nc.vector.tensor_reduce(rt[:, top, :], src[:, :, :], AX.X, ALU.max))
                step(tt(eq[:, :, :], src[:, :, :], bc(rt[:, top, :]), ALU.is_equal))
                step(tt(eq[:, :, :], eq[:, :, :],
                        rank[:, :].rearrange("p (a e) -> p a e", a=1).to_broadcast([128, NT, E]), ALU.mult))
                step(nc.vector.tensor_reduce(rt[:, 7, :], eq[:, :, :], AX.X, ALU.max))
                step(tt(hot[:, :, :], eq[:, :, :], bc(rt[:, 7, :]), ALU.is_equal))

            def moe(k):
                if k == 0:
                    dve.wait_ge(const_ready, CONST)
                    dve.wait_ge(small_loaded, 16 * 6)
                low_parts(k)
                dve.wait_ge(rt_logits, k + 1)
                step(tt(lg[:, :, :], ps[:, 5, 0:NT * E].rearrange("p (t e) -> p t e", e=E),
                        rb[:, :].rearrange("p (a e) -> p a e", a=1).to_broadcast([128, NT, E]), ALU.add))
                pick(lg, best, 0)
                step(stt(lg2[:, :, :], best[:, :, :], EXCLUDE, lg[:, :, :], ALU.mult, ALU.add))
                pick(lg2, second, 1)
                tt(rt[:, 2, :], rt[:, 1, :], rt[:, 0, :], ALU.subtract).then_inc(rt_diff, 1)
                dve.wait_ge(rt_exp, k + 1)
                step(ts(rt[:, 4, :], rt[:, 3, :], 1.0, None, ALU.add))
                step(nc.vector.reciprocal(rt[:, 5, :], rt[:, 4, :]))
                step(tt(rt[:, 6, :], rt[:, 3, :], rt[:, 5, :], ALU.mult))
                step(tt(best[:, :, :], best[:, :, :], bc(rt[:, 5, :]), ALU.mult))
                step(tt(second[:, :, :], second[:, :, :], bc(rt[:, 6, :]), ALU.mult))
                tt(gates[:, :, :], best[:, :, :], second[:, :, :], ALU.add).then_inc(rt_gates, 1)
                if k == 0:
                    dve.wait_ge(w_hi, 1)
                    tt(w1_l[:, :, :], w1_raw, w1_h[:, :, :].bitcast(fp32), ALU.subtract).then_inc(w_lo, 1)
                with dve.Fori(0, NC) as c:
                    at = k * NC + c

                    def low(u):
                        tt(h_l[:, u % 4, :], h_raw[:, u % 4, :], h_h[:, u % 4, :].bitcast(fp32), ALU.subtract).then_inc(h_done, 1)

                    def add_expert(e):
                        dve.wait_ge(w2_done, PRIME + at * UNITS + HT0 * (e + 1))
                        dve.wait_ge(g_loaded[e], 16 * (at + 1))
                        stt(y_gated[:, e % 2, :], ps[:, 4 + e % 2, :], b2[:, e:e + 1], g_bc[:, e, :],
                            ALU.add, ALU.mult).then_inc(y_gate, 1)

                    def finish_expert(e):
                        n = at * E + e
                        dve.wait_ge(y_gate, PRIME + n + 1)
                        if e > 0:
                            dve.wait_ge(y_add, at * (E - 1) + e)
                        stt(x[:, ds(c * CH, CH)], y_gated[:, e % 2, :], 0.5, x[:, ds(c * CH, CH)],
                            ALU.mult, ALU.add).then_inc(y_add if e < E - 1 else x_ready, 1)
                    for u in range(0, UNITS, 2):
                        v = u + 1
                        dve.wait_ge(h_relu, PRIME + at * UNITS + v + 1)
                        dve.wait_ge(w2_done, PRIME + at * UNITS + max(v - 3, 0))
                        nc.vector.tensor_copy(h_h[:, v % 4, :], h_raw[:, v % 4, :]).then_inc(h_hi2, 1)
                        dve.wait_ge(h_hi, at * (UNITS // 2) + u // 2 + 1)
                        low(u)
                        dve.wait_ge(h_hi2, at * (UNITS // 2) + u // 2 + 1)
                        low(v)
                        done = v - LAG - HT0
                        if done >= 0 and (done + 1) % HT0 == 2:
                            add_expert(done // HT0)
                        if done >= 0 and (done + 1) % HT0 == 0:
                            finish_expert(done // HT0)
                    add_expert(E - 2)
                    finish_expert(E - 2)
                    add_expert(E - 1)
                    finish_expert(E - 1)

            def rwkv():
                s = lambda n, off=0: big[:, n, off:off + T]
                for c in range(NC):
                    dve.wait_ge(ln_out, NC + c + 1)
                    step(tt(big[:, 0, chunk(c)], xn[:, chunk(c)], xprev[:, chunk(c)], ALU.subtract))
                    stt(big[:, 2, chunk(c)], big[:, 0, chunk(c)], mix[:, 0:1], xprev[:, chunk(c)], ALU.mult, ALU.add).then_inc(mixed, 1)
                for j in range(1, 3):
                    stt(s(2 + j), s(0), mix[:, j:j + 1], xprev, ALU.mult, ALU.add).then_inc(mixed, 1)
                dve.wait_ge(mixed, NC + 2)
                dve.wait_ge(act_step, 1)
                step(ts(decay[:, 1:2], decay[:, 0:1], -1.0, None, ALU.mult))
                w = decay[:, 1:2]
                k_, r_ = s(5), s(7)
                p, p_next = s(0), s(0, 1)
                step(nc.vector.memset(big[:, 0, 0:1], NO_STATE))
                dve.wait_ge(kvr_done, NC)
                step(nc.vector.tensor_tensor_scan(p_next, w.to_broadcast([C, T]), k_, NO_STATE, ALU.add, ALU.max))
                stt(s(1, 1), p, w, p_next, ALU.add, ALU.subtract).then_inc(wkv_arg, 1)
                dve.wait_ge(kvr_ps, NC * 3)
                tt(s(2, 1), k_, p_next, ALU.subtract).then_inc(wkv_arg, 1)
                step(stt(s(3, 1), k_, mix[:, 4:5], p, ALU.add, ALU.max))
                tt(s(4, 1), p, s(3, 1), ALU.subtract).then_inc(wkv_arg, 1)
                dve.wait_ge(wkv_arg, 3)
                stt(s(3, 1), k_, mix[:, 4:5], s(3, 1), ALU.add, ALU.subtract).then_inc(wkv_arg, 1)
                f1, f2, e1 = s(1, 1), s(2, 1), s(4, 1)
                dve.wait_ge(wkv_arg, 4)
                step(nc.vector.memset(big[:, 0, 0:1], 0.0))
                dve.wait_ge(wkv_exp, 2)
                step(nc.vector.tensor_tensor_scan(s(0, 1), f1, f2, 0.0, ALU.mult, ALU.add))
                step(nc.vector.memset(big[:, 5, 0:1], 0.0))
                dve.wait_ge(wkv_exp, 4)
                step(tt(s(0), e1, s(0), ALU.mult))
                for c in range(NC):
                    cols = slice(1 + c * CH, 1 + c * CH + CH)
                    tt(big[:, 0, chunk(c)], big[:, 0, chunk(c)], big[:, 3, cols], ALU.add).then_inc(wkv_den, 1)
                dve.wait_ge(wkv_prod, 1)
                step(nc.vector.tensor_tensor_scan(s(5, 1), f1, cen[:, :], 0.0, ALU.mult, ALU.add))
                step(tt(s(5), e1, s(5), ALU.mult))
                dve.wait_ge(wkv_prod, 2)
                step(tt(s(5), s(5), sqr[:, :], ALU.add))
                dve.wait_ge(kvr_done, NC * 3)
                step(tt(s(5), s(5), r_, ALU.mult))
                for c in range(NC):
                    cols = chunk(c)
                    d, first_value = big[:, 0, cols], big[:, 2, cols]
                    dve.wait_ge(wkv_inv, c + 1)
                    step(tt(d, d, first_value, ALU.mult))
                    step(stt(d, d, 2.0, first_value, ALU.subtract, ALU.mult))
                    stt(first_value, d, -1.0, big[:, 5, cols], ALU.mult, ALU.mult).then_inc(wkv_out, 1)
                for c in range(NC):
                    dve.wait_ge(o_ps, c + 1)
                    tt(x[:, chunk(c)], x[:, chunk(c)], ps[:, 4 + c, :], ALU.add).then_inc(x_ready, 1)

            def quant_ffn(k):
                low_parts(2 * k + 2)

                def add_down(c):
                    dve.wait_ge(f_down, PRIME + k * NC + c + 1)
                    stt(x[:, chunk(c)], ps[:, 6 + c % 2, :], 0.5 * QUANT_SCALE, x[:, chunk(c)],
                        ALU.mult, ALU.add).then_inc(x_ready, 1)

                for c in range(NC):
                    for ht in range(HT1):
                        n = (k * NC + c) * HT1 + ht
                        dve.wait_ge(f_sigmoid, n + 1)
                        stt(f_sig[:, ht, :], ps[:, 2 * ht, :], QUANT_SCALE, f_sig[:, ht, :], ALU.mult, ALU.mult).then_inc(f_silu, 1)
                        dve.wait_ge(f_silu, n + 1)
                        if n >= HT1:
                            dve.wait_ge(f_lo, n + 1 - HT1)
                        stt(f_hid[:, ht, :], ps[:, 2 * ht + 1, :], QUANT_SCALE, f_sig[:, ht, :], ALU.mult, ALU.mult).then_inc(f_prod, 1)
                    if c > 0:
                        add_down(c - 1)
                add_down(NC - 1)

            def rms_norm():
                for c in range(NC + 1):
                    if c < NC:
                        tiles = slice(TPC * c, TPC * c + TPC)
                        dve.wait_ge(rms_std, c + 1)
                        step(ts(ln_s[:, tiles], ln_s[:, tiles], RMS_EPS, None, ALU.max))
                        nc.vector.reciprocal(ln_r[:, tiles], ln_s[:, tiles]).then_inc(rms_rec, 1)
                    if c > 0:
                        done = chunk(c - 1)
                        dve.wait_ge(rms_bc, c)
                        stt(xn[:, done], xn[:, done], gamma1[:, 0:1], ps[:, c - 1, :], ALU.mult, ALU.mult).then_inc(rms_out, 1)

            def low_qk_weights(par, head):
                dve.wait_ge(qkw_hi, head + 1)
                tt(qk_l[par][:, :, :], qk_raw[par][:, :, :], qk_h[par][:, :, :].bitcast(fp32), ALU.subtract).then_inc(qkw_lo, 1)

            def low_v_weights(pair):
                dve.wait_ge(vw_hi, pair + 1)
                tt(wv_hl[:, 1, :], wv_raw[:, :], wv_hl[:, 0, :].bitcast(fp32), ALU.subtract).then_inc(vw_lo, 1)

            def low_qk(head, par, c, bank):
                n = 12 * head + 3 * c
                cols = chunk(c)
                dve.wait_ge(hi_done, n + 1)
                stt(qb[par][0:DH, cols], ps[0:DH, bank, :], SCORE_SCALE, qa[par][0:DH, cols].bitcast(fp32),
                    ALU.mult, ALU.subtract).then_inc(lo_done, 1)
                dve.wait_ge(hi_done, n + 2)
                tt(ka[par][0:DH, cols], ps[DH:128, bank, :], ka[par][DH:128, cols].bitcast(fp32),
                   ALU.subtract).then_inc(lo_done, 1)
                nc.vector.tensor_copy(kb[par][0:DH, cols], ka[par][DH:128, cols].bitcast(fp32)).then_inc(kb_done, 1)

            def sum_v(pair, b, bank):
                dve.wait_ge(v_ps, V_STEPS * pair + b + 1)
                if b == 0 and not (isinstance(pair, int) and pair == 0):
                    dve.wait_ge(v_lo, 2 * pair)
                nc.vector.tensor_reduce(v_raw[:, 2 * b:2 * b + 2, :], ps[:, bank, :].rearrange("p (t a d) -> p t d a", t=2, a=2),
                                        AX.X, ALU.add).then_inc(v_sum, 1)

            def maximum(head, c, it):
                dve.wait_ge(s_ps, NC * NT * head + NT * c + it + 1)
                nc.vector.tensor_reduce(m_part[:, ds(c, 1), it:it + 1].rearrange("p a t -> p (a t)"),
                                        ps[:, 4 + it % 2, :], AX.X, ALU.max).then_inc(s_max, 1)

            def maxima_end(head, par):
                dve.wait_ge(s_max, PRIME + NC * NT * (head + 1))
                nc.vector.tensor_reduce(m_col[par][:, :], m_part[:, :, :].rearrange("p c t -> p t c"),
                                        AX.X, ALU.max, negate=True).then_inc(m_ready, 1)

            def outputs(head, par, c):
                rows = slice(par * DH, par * DH + DH)
                if not (isinstance(head, int) and head < 2):
                    dve.wait_ge(o_scaled, PRIME + NC * (head - 1))
                dve.wait_ge(pv_done, GROUPS * (NC * head + c + 1))
                nc.vector.tensor_copy(o_raw[rows, chunk(c)], ps[0:DH, sums_bank(c), :]).then_inc(o_done, 1)

            def invert(head, par):
                dve.wait_ge(l_loaded, 16 * (head + 1))
                nc.vector.reciprocal(r_col[:, par, :], l_col[:, par, :]).then_inc(r_ready, 1)

            def add_out(pair, c, bank):
                dve.wait_ge(out_ps, PRIME + NC * pair + c + 1)
                tt(x[:, ds(c * CH, CH)], x[:, ds(c * CH, CH)], ps[:, bank, :], ALU.add).then_inc(out_add, 1)

            def low_part(head, c, g, start):
                if g not in POOL_GROUPS:
                    n = GROUPS * (NC * head + c) + g
                    dve.wait_ge(ph_done, n + 1)
                    if not start or g >= 4:
                        dve.wait_ge(pv_done, n - 3)
                    tt(p_l[:, g % 4, 0, :], p_raw[:, g % 4, 0, :], p_h[:, g % 4, 0, :].bitcast(fp32),
                       ALU.subtract).then_inc(pl_even, 1)

            def end_scale(c):
                rows = slice(DH, 2 * DH)
                dve.wait_ge(end_l, c + 1)
                dve.wait_ge(o_scaled, PRIME + NC * (HEADS - 2))
                nc.vector.reciprocal(r_bc[rows, chunk(c)], ps[rows, 4, :]).then_inc(end_r, 1)
                dve.wait_ge(end_r, c + 1)
                dve.wait_ge(o_done, PRIME + NC * (HEADS - 1) + c + 1)
                dve.wait_ge(out_ps, PRIME + NC * (PAIRS - 2) + c + 1)
                tt(o_nrm[rows, chunk(c)], o_raw[rows, chunk(c)], r_bc[rows, chunk(c)], ALU.mult).then_inc(end_o, 1)

            def end_add(c):
                dve.wait_ge(end_ps, c + 1)
                dve.wait_ge(out_add, PRIME + NC * (PAIRS - 2) + c + 1)
                tt(x[:, chunk(c)], x[:, chunk(c)], ps[:, 5, :], ALU.add).then_inc(x_ready, 1)

            def main_chunk(pair, par, c, with_next, project, with_out, invert_before):
                head = 2 * pair + par
                start = first_of_all(pair, par, c)
                tiles = iter(range(NT))
                for g in range(GROUPS):
                    if g > 0:
                        low_part(head, c, g - 1, start)
                    elif c > 0:
                        low_part(head, c - 1, GROUPS - 1, False)
                    elif not start:
                        low_part(head - 1, NC - 1, GROUPS - 1, False)
                    if with_next:
                        for _ in range(MAXIMA_TILES[c][g]):
                            maximum(head + 1, c, next(tiles))
                        if (c, g) == (NC - 1, GROUPS - 2):
                            maxima_end(head + 1, 1 - par)
                    if g == PV_LAG and not start:
                        if c > 0:
                            outputs(head, par, c - 1)
                        else:
                            outputs(head - 1, 1 - par, NC - 1)
                    if (c, g) == (0, GROUPS - 1) and invert_before:
                        invert(head - 1, 1 - par)
                    n = PROJECTED.get((c, g)) if project else None
                    if n is not None:
                        low_qk(head + 2, par, n, spare_bank(c))
                    b = V_AT[par].get((c, g)) if project else None
                    if b is not None:
                        sum_v(pair + 1, b, spare_bank(c))
                    if with_out and g == OUT_GROUP[c]:
                        add_out(pair - 1, c, spare_bank(c))
                    if not with_next and par == 1 and c > 0 and g == END_GROUPS[1]:
                        end_scale(c - 1)
                    if not with_next and par == 1 and c > 0 and g == END_GROUPS[2]:
                        end_add(c - 1)

            def window(pair, par, with_next, project):
                head = 2 * pair + par
                later = not (isinstance(pair, int) and pair == 0)
                with_out = par == 1 and later
                main_chunk(pair, par, 0, with_next, project, with_out, later or par == 1)
                if project:
                    low_qk_weights(par, head + 2)
                    if par == 0:
                        low_v_weights(pair + 1)
                for c in range(1, NC):
                    main_chunk(pair, par, c, with_next, project, with_out, False)
                if project:
                    low_qk(head + 2, par, NC - 1, END_BANK)

            def attention():
                low_parts(3)
                for head in range(2):
                    low_qk_weights(head, head)
                low_v_weights(0)
                for head in range(2):
                    for c in range(NC):
                        low_qk(head, head, c, NC * head + c)
                for b in range(V_STEPS):
                    sum_v(0, b, b % 4)
                for it in range(NT):
                    dve.wait_ge(s_ps, NC * (it + 1))
                    nc.vector.tensor_reduce(m_part[:, 0, it:it + 1], ps[:, 4 * ((it + 1) % 2):4 * ((it + 1) % 2) + 4, :].rearrange("p b n -> p (b n)"),
                                            AX.X, ALU.max).then_inc(s_max, NC)
                dve.wait_ge(s_max, PRIME + NC * NT)
                ts(m_col[0][:, :], m_part[:, 0, :], -1.0, None, ALU.mult).then_inc(m_ready, 1)
                window(0, 0, True, True)
                window(0, 1, True, True)
                with dve.Fori(1, PAIRS - 1) as pair:
                    window(pair, 0, True, True)
                    window(pair, 1, True, True)
                window(PAIRS - 1, 0, True, False)
                window(PAIRS - 1, 1, False, False)
                low_part(HEADS - 1, NC - 1, GROUPS - 1, False)
                outputs(HEADS - 1, 1, NC - 1)
                end_scale(NC - 1)
                end_add(NC - 1)

            layer_norm(0)
            moe(0)
            layer_norm(1)
            rwkv()
            layer_norm(2)
            moe(1)
            layer_norm(3)
            dve.wait_ge(l1_loaded, 16 * 3)
            nc.vector.tensor_copy(wgu[:, :, :], wgu_i).then_inc(dequantised, 1)
            nc.vector.tensor_copy(wd[:, :, :], wd_i).then_inc(dequantised, 1)
            step(ts(gamma1[:, :], gamma1[:, :], 1.0, float(C) ** 0.5, ALU.add, ALU.mult))
            quant_ffn(0)
            layer_norm(4)
            rms_norm()
            attention()
            layer_norm(5)
            quant_ffn(1)


def kernel(**inputs):
    import numpy as np
    import concourse.bacc as bacc
    from concourse.bass_utils import run_bass_kernel_spmd

    g = {n: np.asarray(v) for n, v in inputs.items()}
    laid = {
        "xT": g["L0_attn_x"][0].T,
        "router_w": g["L0_ffn_router_w"],
        "router_b": g["L0_ffn_router_b"],
        "w1T": g["L0_ffn_w1"].transpose(1, 0, 2),
        "b1T": g["L0_ffn_b1"].reshape(E, HT0, 128).transpose(2, 0, 1),
        "w2T": g["L0_ffn_w2"].reshape(E, HT0, 128, C).transpose(2, 0, 1, 3),
        "b2T": g["L0_ffn_b2"].T,
        "rwkv_wT": np.stack([g["L0_attn_" + n].T for n in ("Wk", "Wv", "Wr", "Wo")], axis=1),
        "mix": np.stack([g["L0_attn_" + n].reshape(C) for n in
                         ("time_mix_k", "time_mix_v", "time_mix_r", "time_decay", "time_first")], axis=1),
        "gamma": g["L1_attn_gamma"].reshape(C, 1),
        "w_qkv": g["L1_attn_w_qkv"],
        "w_out": g["L1_attn_w_out"],
        "w_gate_upT": np.stack([g["L1_ffn_w_gate"].T, g["L1_ffn_w_up"].T], axis=1),
        "w_downT": g["L1_ffn_w_down"].T.reshape(HT1, 128, C).transpose(1, 0, 2),
    }
    nc = bacc.Bacc("TRN2", target_bir_lowering=False, num_devices=1)
    arrays, aps = {}, {}
    for name, v in laid.items():
        v = np.ascontiguousarray(v)
        arrays[f"in_{name}"] = v
        aps[name] = nc.dram_tensor(f"in_{name}", v.shape, mybir.dt.from_np(v.dtype), kind="ExternalInput").ap()
    out = nc.dram_tensor("out_xT", (C, T), fp32, kind="ExternalOutput").ap()
    g_scratch = nc.dram_tensor("g_scratch", (2, E, T), fp32, kind="Internal").ap()
    l_scratch = nc.dram_tensor("l_scratch", (HEADS, T), fp32, kind="Internal").ap()
    r_scratch = nc.dram_tensor("r_scratch", (HEADS, T), fp32, kind="Internal").ap()
    macaron_kernel(nc, aps, out, g_scratch, l_scratch, r_scratch)
    r = run_bass_kernel_spmd(nc, [arrays], core_ids=[0])
    return np.ascontiguousarray(r.results[0]["out_xT"].T).reshape(1, T, C)
```
